# Optimizing a Trainium2 kernel written in Bass

```python
import numpy as np
import jax
import jax.numpy as jnp

def _softmax(x, axis=-1):
    return jax.nn.softmax(x, axis=axis)

def _gelu(x):
    return jax.nn.gelu(x, approximate=True)

def _silu(x):
    return jax.nn.silu(x)

def _sigmoid(x):
    return jax.nn.sigmoid(x)

def _layernorm(x, axis=-1, eps=1e-05):
    m = jnp.mean(x, axis=axis, keepdims=True)
    v = jnp.var(x, axis=axis, keepdims=True)
    return (x - m) / jnp.sqrt(v + eps)

def _scatter_add(tgt, idx, src, axis=0):
    return tgt.at[idx].add(src)

def _segment_sum(src, seg, n):
    return jax.ops.segment_sum(src, seg, n)
kernel_name = 'mk_decoder_postln_d1_seqx_r8_d112e0'

def setup_inputs(seed: int=0):
    np.random.seed(seed)
    _w = jnp.asarray

    def _rec_inputs():
        import jax
        import jax.numpy as jnp
        _rk = jax.random.key(seed)
        x = 7.22e-05 + 1 * jax.random.normal(jax.random.fold_in(_rk, 1), (4, 256, 128), jnp.float32)
        _lenS = 256 - jax.random.randint(jax.random.fold_in(_rk, 7), (4,), 0, max(1, 256 // 4) + 1, jnp.int32)
        _lenS2 = 256 - jax.random.randint(jax.random.fold_in(_rk, 8), (4,), 0, max(1, 256 // 4) + 1, jnp.int32)
        _ctx_1024P = jax.random.normal(jax.random.fold_in(_rk, 11), (4, 16, 128), jnp.float32)
        _ctx_1024c = jax.random.dirichlet(jax.random.fold_in(_rk, 511), 0.3 * jnp.ones((16,), jnp.float32), (4, 256))
        _ctx_1024t = jnp.einsum('bsk,bkd->bsd', _ctx_1024c, _ctx_1024P)
        _ctx_1024t = _ctx_1024t * jax.lax.rsqrt(jnp.mean(jnp.square(_ctx_1024t)) + 1e-12) * 0.953939
        ctx_1024 = 4.13588e-05 + 0.999923 * (_ctx_1024t + 0.3 * jax.random.normal(jax.random.fold_in(_rk, 611), (4, 256, 128), jnp.float32))
        _validS = jnp.arange(256)[None, :] < _lenS[:, None]
        _validS2 = jnp.arange(256)[None, :] < _lenS2[:, None]
        _causal = jnp.tril(jnp.ones((256, 256), dtype=bool))
        mask_BxSxS2_if1 = jnp.where(jnp.ones((4, 256, 256), dtype=bool), 1, 0).astype(jnp.int32)
        return (x, ctx_1024, mask_BxSxS2_if1)
    x, ctx_1024, mask_BxSxS2_if1 = _rec_inputs()

    def _L0_attn_setup():
        import jax, jax.numpy as jnp
        import numpy as np
        import math
        D_MODEL = 128
        N_HEADS = 16
        D_K = D_MODEL // N_HEADS
        MAX_REL = 32
        key = jax.random.key(seed)
        ks = jax.random.split(key, 8)
        B, S = (8, 128)
        x = jax.random.normal(ks[0], (B, S, D_MODEL), dtype=jnp.float32)
        scale = 1.0 / math.sqrt(D_MODEL)
        Wq = jax.random.normal(ks[1], (D_MODEL, D_MODEL), dtype=jnp.float32) * scale
        Wk = jax.random.normal(ks[2], (D_MODEL, D_MODEL), dtype=jnp.float32) * scale
        Wv = jax.random.normal(ks[3], (D_MODEL, D_MODEL), dtype=jnp.float32) * scale
        Wo = jax.random.normal(ks[4], (D_MODEL, D_MODEL), dtype=jnp.float32) * scale
        b_o = jnp.zeros((D_MODEL,), dtype=jnp.float32)
        rel_k_emb = jax.random.normal(ks[5], (2 * MAX_REL + 1, D_K), dtype=jnp.float32) * 0.02
        rel_v_emb = jax.random.normal(ks[6], (2 * MAX_REL + 1, D_K), dtype=jnp.float32) * 0.02
        return {'x': x, 'Wq': Wq, 'Wk': Wk, 'Wv': Wv, 'Wo': Wo, 'b_o': b_o, 'rel_k_emb': rel_k_emb, 'rel_v_emb': rel_v_emb}
    _L0_attn_all = _L0_attn_setup()
    _L0_attn_in = {k: v for k, v in _L0_attn_all.items() if k in ('Wq', 'Wk', 'Wv', 'Wo', 'b_o', 'rel_k_emb', 'rel_v_emb')}
    del _L0_attn_all

    def _L0_xattn_setup():
        import jax, jax.numpy as jnp
        import numpy as np
        B, S, H = (4, 256, 128)
        key = jax.random.key(seed)
        ks = jax.random.split(key, 12)
        scale = 1.0 / np.sqrt(H)
        inp = {'query': jax.random.normal(ks[0], (B, S, H), jnp.float32), 'key': jax.random.normal(ks[1], (B, S, H), jnp.float32), 'value': jax.random.normal(ks[2], (B, S, H), jnp.float32), 'mask': jnp.ones((B, S, S), jnp.int32), 'Wq': jax.random.normal(ks[3], (H, H), jnp.float32) * scale, 'bq': jnp.zeros((H,), jnp.float32), 'Wk': jax.random.normal(ks[4], (H, H), jnp.float32) * scale, 'bk': jnp.zeros((H,), jnp.float32), 'Wv': jax.random.normal(ks[5], (H, H), jnp.float32) * scale, 'bv': jnp.zeros((H,), jnp.float32), 'Wo': jax.random.normal(ks[6], (H, H), jnp.float32) * scale, 'bo': jnp.zeros((H,), jnp.float32)}
        return inp
    _L0_xattn_all = _L0_xattn_setup()
    _L0_xattn_in = {k: v for k, v in _L0_xattn_all.items() if k in ('Wq', 'bq', 'Wk', 'bk', 'Wv', 'bv', 'Wo', 'bo')}
    del _L0_xattn_all

    def _L0_ffn_setup():
        import jax, jax.numpy as jnp
        import numpy as np
        D_IN, D_HID = (128, 512)

        def _ternary(key, shape):
            return jax.random.randint(key, shape, -1, 2).astype(jnp.float32)

        def _tlin(x, w, s):
            return jnp.einsum('bsi,oi->bso', x, w) * s
        key = jax.random.key(seed)
        ks = jax.random.split(key, 12)
        inv = lambda fan: 1.0 / np.sqrt(fan).astype(np.float32)
        return {'x': jax.random.normal(ks[0], (4, 256, D_IN), dtype=jnp.float32), 'w1_w': _ternary(ks[1], (D_HID, D_IN)), 'w1_s': jax.random.uniform(ks[2], (D_HID,), dtype=jnp.float32) * inv(D_IN), 'w2_w': _ternary(ks[3], (D_HID, D_IN)), 'w2_s': jax.random.uniform(ks[4], (D_HID,), dtype=jnp.float32) * inv(D_IN), 'h1_w': _ternary(ks[5], (D_HID, D_HID)), 'h1_s': jax.random.uniform(ks[6], (D_HID,), dtype=jnp.float32) * inv(D_HID), 'h2_w': _ternary(ks[7], (D_HID, D_HID)), 'h2_s': jax.random.uniform(ks[8], (D_HID,), dtype=jnp.float32) * inv(D_HID), 'w3_w': _ternary(ks[9], (D_IN, D_HID)), 'w3_s': jax.random.uniform(ks[10], (D_IN,), dtype=jnp.float32) * inv(D_HID)}
    _L0_ffn_all = _L0_ffn_setup()
    _L0_ffn_in = {k: v for k, v in _L0_ffn_all.items() if k in ('w1_w', 'w1_s', 'w2_w', 'w2_s', 'h1_w', 'h1_s', 'h2_w', 'h2_s', 'w3_w', 'w3_s')}
    del _L0_ffn_all
    return {'x': x, 'ctx_1024': ctx_1024, 'mask_BxSxS2_if1': mask_BxSxS2_if1, 'L0_attn_Wq': _L0_attn_in['Wq'], 'L0_attn_Wk': _L0_attn_in['Wk'], 'L0_attn_Wv': _L0_attn_in['Wv'], 'L0_attn_Wo': _L0_attn_in['Wo'], 'L0_attn_b_o': _L0_attn_in['b_o'], 'L0_attn_rel_k_emb': _L0_attn_in['rel_k_emb'], 'L0_attn_rel_v_emb': _L0_attn_in['rel_v_emb'], 'L0_xattn_Wq': _L0_xattn_in['Wq'], 'L0_xattn_bq': _L0_xattn_in['bq'], 'L0_xattn_Wk': _L0_xattn_in['Wk'], 'L0_xattn_bk': _L0_xattn_in['bk'], 'L0_xattn_Wv': _L0_xattn_in['Wv'], 'L0_xattn_bv': _L0_xattn_in['bv'], 'L0_xattn_Wo': _L0_xattn_in['Wo'], 'L0_xattn_bo': _L0_xattn_in['bo'], 'L0_ffn_w1_w': _L0_ffn_in['w1_w'], 'L0_ffn_w1_s': _L0_ffn_in['w1_s'], 'L0_ffn_w2_w': _L0_ffn_in['w2_w'], 'L0_ffn_w2_s': _L0_ffn_in['w2_s'], 'L0_ffn_h1_w': _L0_ffn_in['h1_w'], 'L0_ffn_h1_s': _L0_ffn_in['h1_s'], 'L0_ffn_h2_w': _L0_ffn_in['h2_w'], 'L0_ffn_h2_s': _L0_ffn_in['h2_s'], 'L0_ffn_w3_w': _L0_ffn_in['w3_w'], 'L0_ffn_w3_s': _L0_ffn_in['w3_s']}

def reference(x, ctx_1024, mask_BxSxS2_if1, L0_attn_Wq, L0_attn_Wk, L0_attn_Wv, L0_attn_Wo, L0_attn_b_o, L0_attn_rel_k_emb, L0_attn_rel_v_emb, L0_xattn_Wq, L0_xattn_bq, L0_xattn_Wk, L0_xattn_bk, L0_xattn_Wv, L0_xattn_bv, L0_xattn_Wo, L0_xattn_bo, L0_ffn_w1_w, L0_ffn_w1_s, L0_ffn_w2_w, L0_ffn_w2_s, L0_ffn_h1_w, L0_ffn_h1_s, L0_ffn_h2_w, L0_ffn_h2_s, L0_ffn_w3_w, L0_ffn_w3_s):
    import jax
    import jax.numpy as jnp

    def _L0_attn_ref(x, Wq, Wk, Wv, Wo, b_o, rel_k_emb, rel_v_emb):
        import jax, jax.numpy as jnp
        import numpy as np
        import math
        D_MODEL = 128
        N_HEADS = 16
        D_K = D_MODEL // N_HEADS
        MAX_REL = 32
        B, S, D = x.shape
        H, dk = (N_HEADS, D_K)
        inv_sqrt_dk = 1.0 / math.sqrt(dk)
        Q = (x @ Wq.T).reshape(B, S, H, dk)
        K = (x @ Wk.T).reshape(B, S, H, dk)
        V = (x @ Wv.T).reshape(B, S, H, dk)
        pos = jnp.arange(S)
        rel_idx = jnp.clip(pos[None, :] - pos[:, None], -MAX_REL, MAX_REL) + MAX_REL
        rel_k = rel_k_emb[rel_idx]
        rel_v = rel_v_emb[rel_idx]
        scores = jnp.einsum('bihd,bjhd->bhij', Q, K) * inv_sqrt_dk
        scores = scores + jnp.einsum('bihd,ijd->bhij', Q, rel_k) * inv_sqrt_dk
        attn = jax.nn.softmax(scores, axis=-1)
        ctx = jnp.einsum('bhij,bjhd->bihd', attn, V)
        ctx = ctx + jnp.einsum('bhij,ijd->bihd', attn, rel_v)
        ctx = ctx.reshape(B, S, D)
        out = ctx @ Wo.T + b_o
        return out

    def _L0_xattn_ref(query, key, value, mask, Wq, bq, Wk, bk, Wv, bv, Wo, bo):
        import jax, jax.numpy as jnp
        import numpy as np
        B, S, H = (4, 256, 128)
        q = jnp.einsum('bsh,oh->bso', query, Wq) + bq
        k = jnp.einsum('bsh,oh->bso', key, Wk) + bk
        v = jnp.einsum('bsh,oh->bso', value, Wv) + bv
        scores = jnp.einsum('bqh,bkh->bqk', q, k) / jnp.sqrt(jnp.float32(H))
        scores = jnp.where(mask == 0, jnp.float32(-1000000000.0), scores)
        attn = jax.nn.softmax(scores, axis=-1)
        context = jnp.einsum('bqk,bkh->bqh', attn, v)
        out = jnp.einsum('bqh,oh->bqo', context, Wo) + bo
        return out

    def _L0_ffn_ref(x, w1_w, w1_s, w2_w, w2_s, h1_w, h1_s, h2_w, h2_s, w3_w, w3_s):
        import jax, jax.numpy as jnp
        import numpy as np
        D_IN, D_HID = (128, 512)

        def _ternary(key, shape):
            return jax.random.randint(key, shape, -1, 2).astype(jnp.float32)

        def _tlin(x, w, s):
            return jnp.einsum('bsi,oi->bso', x, w) * s
        h = jax.nn.silu(_tlin(x, w1_w, w1_s)) * _tlin(x, w2_w, w2_s)
        h = jax.nn.gelu(_tlin(h, h1_w, h1_s), approximate=False)
        h = jax.nn.gelu(_tlin(h, h2_w, h2_s), approximate=False)
        return _tlin(h, w3_w, w3_s)
    x = _layernorm(x + _L0_attn_ref(x, L0_attn_Wq, L0_attn_Wk, L0_attn_Wv, L0_attn_Wo, L0_attn_b_o, L0_attn_rel_k_emb, L0_attn_rel_v_emb), axis=-1)
    x = _layernorm(x + _L0_xattn_ref(x, ctx_1024, ctx_1024, mask_BxSxS2_if1, L0_xattn_Wq, L0_xattn_bq, L0_xattn_Wk, L0_xattn_bk, L0_xattn_Wv, L0_xattn_bv, L0_xattn_Wo, L0_xattn_bo), axis=-1)
    x = _layernorm(x + _L0_ffn_ref(x, L0_ffn_w1_w, L0_ffn_w1_s, L0_ffn_w2_w, L0_ffn_w2_s, L0_ffn_h1_w, L0_ffn_h1_s, L0_ffn_h2_w, L0_ffn_h2_s, L0_ffn_w3_w, L0_ffn_w3_s), axis=-1)
    return x

_drawn_inputs = setup_inputs


def setup_inputs(seed=0):
    import zlib

    import numpy as np

    out = dict(_drawn_inputs(seed))
    spreads = {'L0_attn_b_o': (0.0, 0.1),
     'L0_xattn_bq': (0.0, 0.33),
     'L0_xattn_bk': (0.0, 0.8),
     'L0_xattn_bv': (0.0, 0.1),
     'L0_xattn_bo': (0.0, 0.1)}
    factors = {'L0_attn_rel_k_emb': 8.0,
     'L0_attn_rel_v_emb': 4.058,
     'L0_ffn_w1_w': 8.0,
     'L0_ffn_w1_s': 8.0,
     'L0_ffn_w2_w': 8.0,
     'L0_ffn_w2_s': 8.0,
     'L0_ffn_h1_w': 8.0,
     'L0_ffn_h1_s': 8.0,
     'L0_ffn_h2_w': 8.0,
     'L0_ffn_h2_s': 8.0,
     'L0_ffn_w3_w': 8.0,
     'L0_ffn_w3_s': 8.0}
    for name, (base, spread) in spreads.items():
        noise = np.random.default_rng([zlib.crc32(name.encode()), seed]).standard_normal(out[name].shape)
        drawn = base * np.exp(spread * noise) if base else spread * noise
        out[name] = jnp.asarray(drawn.astype(out[name].dtype))
    for name, factor in factors.items():
        out[name] = (out[name] * factor).astype(out[name].dtype)
    return out
```

```python
from contextlib import ExitStack

import concourse.bass as bass
from concourse import mybir

F32 = mybir.dt.float32
F32R = mybir.dt.float32r
I32 = mybir.dt.int32
ALU = mybir.AluOpType
ACT = mybir.ActivationFunctionType
AX = mybir.AxisListType

P = 128
B, S, D = 4, 256, 128
H, DK = 16, 8
G, K4 = 4, 4
TOK = B * S
NT = TOK // P
HID = 512
NO = HID // P
MAX_REL = 32
NREL = 2 * MAX_REL + 1
BLK = 64
WIN = [0, 32, 96, 128]
VWIN = WIN + [(w + P) % S for w in WIN]
EPS = 1e-5
NEG = -1.0e9
HALO = 384
BH = B * H
VC = DK + 1

QA, QB, KA, KB, KC = range(P, P + 5)


def build(nc, x, xT, ctxT, mask, consts, wqr, wkr, wvT, woT, b_o, relk, relv, relv_far,
          xwq, xbq, xwk, xbk, xwv, xbv, xwo, xbo,
          w1, s1, w2, s2, h1, hs, h2, w3, s3, out):
    with ExitStack() as ctx:
        def sb(name, shape, dt=F32, stack=ctx):
            return stack.enter_context(nc.sbuf_tensor(name, shape, dt))

        def sem(name):
            return ctx.enter_context(nc.semaphore(name))

        ps = ctx.enter_context(nc.psum_tensor("ps", [P, 8, 512], F32))

        con = sb("con", [P, P + 8])
        ident = con[:, 0:P]
        x_nat = sb("x_nat", [P, NT, D])
        ctx_sb = sb("ctx_sb", [P, TOK])
        wo_sb = sb("wo_sb", [P, D])
        xw_sb = sb("xw_sb", [P, 4, D])
        rows = sb("rows", [P, 4, D])
        cols = sb("cols", [P, 2 + 4 * NO])
        near = sb("near", [P, S, BH])
        rv = sb("rv", [P, P, DK])
        pvs = sb("pvs", [P, 2, BH, VC])
        half_pow = sb("half_pow", [P, NT])
        mv = sb("mv", [P, 3, NT, 2])
        rstd = sb("rstd", [P, 3, NT])
        stats = sb("stats", [P, NT, 6])

        early = ExitStack()
        xT_sb = sb("xT_sb", [P, B, HALO], stack=early)
        wv_sb = sb("wv_sb", [P, D], stack=early)
        relraw = sb("relraw", [P, 2 * P], stack=early)
        table_t = sb("table_t", [P, 2 * P], stack=early)
        table_hi = sb("table_hi", [P, 2 * P], F32R, stack=early)
        table = sb("table", [P, 2 * P], F32R, stack=early)
        rvfar = sb("rvfar", [P, 4, DK], stack=early)
        kbias = sb("kbias", [P, 2], stack=early)
        q_st = sb("q_st", [P, K4, TOK], F32R, stack=early)
        k_st = sb("k_st", [P, K4, B, 2 * S], F32R, stack=early)
        q_cut = sb("q_cut", [P, B, H, BLK], F32R, stack=early)
        vw = sb("vw", [P, B, 8, H, VC], stack=early)
        with ExitStack() as projecting:
            wqr_sb = sb("wqr_sb", [P, K4, P], stack=projecting)
            wkr_sb = sb("wkr_sb", [P, K4, P], stack=projecting)
            raw = sb("raw", [P, 2, 512], stack=projecting)
            hi = sb("hi", [P, 2, 2, 512], F32R, stack=projecting)
            part = sb("part", [P, 2, 2, 512], stack=projecting)
        far = sb("far", [P, 2, 512], stack=early)
        mq = sb("mq", [P, 2, B, H], stack=early)
        mr = sb("mr", [P, 2, B, H], stack=early)
        negm = sb("negm", [P, 2, B, H], stack=early)
        negm_hi = sb("negm_hi", [P, 2, B, H], F32R, stack=early)
        negm_st = sb("negm_st", [P, 2, B, 2 * H], stack=early)
        mt = sb("mt", [2 * H, B, S], F32R, stack=early)
        early.close()

        mask_sb = sb("mask_sb", [P, NT, S], I32)
        w1_sb = sb("w1_sb", [P, HID])
        w2_sb = sb("w2_sb", [P, HID])
        h1_sb = sb("h1_sb", [P, NO, HID])
        h2_sb = sb("h2_sb", [P, NO, HID])
        w3_sb = sb("w3_sb", [P, NO, D])
        rvo = sb("rvo", [BH, S, DK])
        lsum = sb("lsum", [P, 2, BH])
        num = sb("num", [P, 2, BH, DK])
        catt = sb("catt", [P, 2, BH, DK])
        cattT = sb("cattT", [P, TOK])
        y = sb("y", [P, NT, D])
        xb = sb("xb", [P, NT, D])
        xn = sb("xn", [P, 3, NT, D])
        xnT = sb("xnT", [P, 2, TOK])
        qT = sb("qT", [P, TOK])
        kT = sb("kT", [P, TOK])
        v_nat = sb("v_nat", [P, NT, D])
        keep = sb("keep", [P, NT, S])
        pen = sb("pen", [P, NT, S])
        sc = sb("sc", [P, NT, S])
        smax = sb("smax", [P, NT])
        ssum = sb("ssum", [P, NT])
        srec = sb("srec", [P, NT])
        silu = sb("silu", [P, 2, 512])
        flat = near[:, :, :].rearrange("p i m -> p (i m)")
        hid = flat[:, 0:3 * NO * TOK].rearrange("p (l o t) -> p l o t", l=3, o=NO)
        rest = 3 * NO * TOK
        pT = flat[:, rest:rest + 2 * TOK].rearrange("p (t j i) -> p t j i", t=NT, j=2)
        cT = flat[:, rest + 2 * TOK:rest + 3 * TOK]

        ld_first, ld_mid, ld_late = sem("ld_first"), sem("ld_mid"), sem("ld_late")
        ld_weights = sem("ld_weights")
        proj_ready, proj_read, split_done = sem("proj_ready"), sem("proj_read"), sem("split_done")
        part_done = sem("part_done")
        dve_step = sem("dve_step")
        ones_set, v_ready = sem("ones_set"), sem("v_ready")
        v_copied = [sem("v_copied_win"), sem("v_copied_far")]
        table_done = sem("table_done")
        cut_done = [sem(f"cut_done{n}") for n in range(2)]
        rel_ready, rel_copied = sem("rel_ready"), sem("rel_copied")
        nat_ready, nat_read = sem("nat_ready"), sem("nat_read")
        dist_ready, dist_read = sem("dist_ready"), sem("dist_read")
        negm_done, negm_turned, negm_copied = sem("negm_done"), sem("negm_turned"), sem("negm_copied")
        shift_placed = [sem(f"shift_placed{b}") for b in range(B)]
        near_ready, far_ready, near_added = sem("near_ready"), sem("far_ready"), sem("near_added")
        exp_near, exp_far = sem("exp_near"), sem("exp_far")
        pv_done, pv_ready, pv_copied = sem("pv_done"), sem("pv_ready"), sem("pv_copied")
        relv_ready, relv_even, relv_odd = sem("relv_ready"), sem("relv_even"), sem("relv_odd")
        relv_turned, catt_done = sem("relv_turned"), sem("catt_done")
        cattT_ready, cattT_copied = sem("cattT_ready"), sem("cattT_copied")
        kT_ready, kT_copied = sem("kT_ready"), sem("kT_copied")
        xv_ready, xv_copied = sem("xv_ready"), sem("xv_copied")
        att_ready, ln_var, ln_rstd = sem("att_ready"), sem("ln_var"), sem("ln_rstd")
        y_done, pool_step = sem("y_done"), sem("pool_step")
        xn_done, xnT_ready, xnT_copied = sem("xn_done"), sem("xnT_ready"), sem("xnT_copied")
        qT_ready, qT_copied = sem("qT_ready"), sem("qT_copied")
        xs_ready, xs_max, xs_exp, xs_norm = sem("xs_ready"), sem("xs_max"), sem("xs_exp"), sem("xs_norm")
        xs_masked = sem("xs_masked")
        pT_ready, pT_copied = sem("pT_ready"), sem("pT_copied")
        cT_ready, cT_copied = sem("cT_ready"), sem("cT_copied")
        gate_ready, silu_done, gate_done = sem("gate_ready"), sem("silu_done"), sem("gate_done")
        mid1_ready, mid1_done = sem("mid1_ready"), sem("mid1_done")
        mid2_ready, mid2_done = sem("mid2_ready"), sem("mid2_done")
        ffn_ready, stored = sem("ffn_ready"), sem("stored")

        N_FIRST, N_MID, N_LATE, N_WEIGHTS = 5, 5, 14, 6
        NJ = 16
        QK_BANKS = 4

        def group(g):
            return slice(32 * g, 32 * g + 32)

        def units():
            for q in range(B * 2 * G):
                yield q, q // 8, q // G % 2, q % G

        block = ctx.enter_context(nc.Block())

        @block.sync
        def _(sp):
            for dst, src in ((xT_sb, xT), (wqr_sb, wqr), (wkr_sb, wkr), (con, consts), (relraw, relk)):
                sp.dma_start(dst[:], src).then_inc(ld_first, 16)
            for dst, src in ((wv_sb[:], wvT), (wo_sb[:], woT),
                             (x_nat[:], x.rearrange("(t p) d -> p t d", p=P))):
                sp.dma_start(dst, src).then_inc(ld_mid, 16)
            sp.dma_start(rvfar[:], relv_far).then_inc(ld_mid, 16)
            slide = bass.AP(relv.tensor, 0, [[DK, P], [1, P * DK]])
            sp.dma_start(rv[:].rearrange("p o d -> p (o d)"), slide).then_inc(ld_mid, 16)

            for half in range(2):
                sp.wait_ge(split_done, 8 * (half + 1))
                for g in range(G):
                    for blk in range(4):
                        for b in (2 * half, 2 * half + 1):
                            i0 = b * S + blk * BLK
                            sp.dma_start(q_cut[group(blk), b, K4 * g:K4 * g + K4, :].bitcast(F32),
                                         q_st[group(g), :, i0:i0 + BLK].bitcast(F32)).then_inc(cut_done[half], 16)

            late = ((ctx_sb[:], ctxT), (xw_sb[:, 0, :], xwq), (xw_sb[:, 1, :], xwk), (xw_sb[:, 2, :], xwv),
                    (xw_sb[:, 3, :], xwo),
                    (rows[:, 0, :], b_o.partition_broadcast(P)), (rows[:, 1, :], xbv.partition_broadcast(P)),
                    (rows[:, 2, :], xbo.partition_broadcast(P)), (rows[:, 3, :], s3.partition_broadcast(P)),
                    (cols[:, 0:1], xbq), (cols[:, 1:2], xbk),
                    (cols[:, 2:2 + NO], s1), (cols[:, 2 + NO:2 + 2 * NO], s2),
                    (cols[:, 2 + 2 * NO:2 + 4 * NO], hs))
            for dst, src in late:
                sp.dma_start(dst, src).then_inc(ld_late, 16)

            for b in range(B):
                sp.wait_ge(negm_copied, b + 1)
                if b == 0:
                    sp.wait_ge(cut_done[0], 16 * 32)
                    sp.wait_ge(cut_done[1], 16 * 32)
                for k in range(K4):
                    for piece in range(2):
                        sp.dma_start(q_st[3 * DK + piece:P:32, k, b * S:b * S + S].bitcast(F32),
                                     mt[H * piece + k:H * (piece + 1):K4, b, :].bitcast(F32)
                                     ).then_inc(shift_placed[b], 16)

            sp.wait_ge(pv_done, 4 * 8)
            for dst, src in ((mask_sb[:], mask.rearrange("(t p) j -> p t j", p=P)), (w1_sb[:], w1), (w2_sb[:], w2),
                             (h1_sb[:], h1.rearrange("(k p) o -> p k o", p=P)),
                             (h2_sb[:], h2.rearrange("(k p) o -> p k o", p=P)),
                             (w3_sb[:], w3.rearrange("(k p) o -> p k o", p=P))):
                sp.dma_start(dst, src).then_inc(ld_weights, 16)

            sp.wait_ge(xn_done, 3 * NT)
            sp.dma_start(out.rearrange("(t p) d -> p t d", p=P), xn[:, 2]).then_inc(stored, 16)
            sp.wait_ge(stored, 16)

        @block.tensor
        def _(pe):
            mm, turn = nc.tensor.matmul, nc.tensor.transpose

            pe.wait_ge(ld_first, 16 * N_FIRST)
            for n in range(NJ):
                half, k, w = n // 8, n // 2 % 4, (wqr_sb, wkr_sb)[n % 2]
                if n >= QK_BANKS:
                    pe.wait_ge(proj_read, n - QK_BANKS + 1)
                mm(ps[:, n % QK_BANKS, :], w[:, k, :], xT_sb[:, 2 * half:2 * half + 2, 0:S],
                   start=True, stop=True).then_inc(proj_ready, 1)

            pe.wait_ge(ld_mid, 16 * N_MID)
            for n in range(2 * B):
                b, side = n // 2, n % 2
                if n >= 2:
                    pe.wait_ge(v_copied[side], n // 2)
                for w in range(4):
                    j0 = VWIN[4 * side + w]
                    last = mm(ps[:, 4 + n % 2, w * D:(w + 1) * D], xT_sb[:, b, j0:j0 + P], wv_sb[:],
                              start=True, stop=True)
                last.then_inc(v_ready, 1)

            pe.wait_ge(table_done, 1)
            pe.wait_ge(cut_done[0], 16 * 32)
            pe.wait_ge(cut_done[1], 16 * 32)
            for n in range(S // 8):
                bank, blk = 6 + n % 2, 8 * n // BLK
                if n >= 2:
                    pe.wait_ge(rel_copied, n - 1)
                for e in range(8):
                    i = 8 * n + e
                    o = i - WIN[blk]
                    last = mm(ps[:, bank, e * BH:(e + 1) * BH], table[group(blk), P - 1 - o:2 * P - 1 - o],
                              q_cut[group(blk), :, :, i % BLK].rearrange("p b h -> p (b h)"),
                              start=True, stop=True)
                last.then_inc(rel_ready, 1)

            def natural(b, half, g):
                u = (2 * b + half) * G + g
                for pair in range(2):
                    n = 2 * u + pair
                    if n == 0:
                        pe.wait_ge(proj_read, NJ)
                        pe.wait_ge(split_done, NJ)
                    if n >= 2:
                        pe.wait_ge(nat_read, n - 1)
                    for e in range(2):
                        k = 2 * pair + e
                        last = mm(ps[:, n % 2, e * S:(e + 1) * S],
                                  q_st[group(g), k, b * S + half * P:b * S + half * P + P],
                                  k_st[group(g), k, b, S:2 * S], start=True, stop=True)
                    last.then_inc(nat_ready, 1)
                if u >= 1:
                    pe.wait_ge(dist_read, u)
                if half == 0 and g == 0 and b >= 1:
                    pe.wait_ge(negm_copied, b)
                for k in range(K4):
                    last = mm(ps[:, 2, k * 66:k * 66 + 66],
                              q_st[group(g), k, b * S + half * P:b * S + half * P + P],
                              table[group(g), P - 1 - MAX_REL:P - 1 - MAX_REL + 66], start=True, stop=True)
                last.then_inc(dist_ready, 1)

            def turn_maxima(b):
                pe.wait_ge(negm_done, b + 1)
                for half in range(2):
                    last = turn(ps[0:2 * H, 2, half * P:(half + 1) * P], negm_st[:, half, b, :], ident)
                last.then_inc(negm_turned, 1)

            def scores(q, b, half, g):
                if q == 0:
                    pe.wait_ge(v_copied[0], B)
                    pe.wait_ge(v_copied[1], B)
                if q % 8 == 0:
                    pe.wait_ge(shift_placed[b], 16 * 2 * K4)
                if q >= 2:
                    pe.wait_ge(near_added, q - 1)
                    pe.wait_ge(exp_far, q - 1)
                for what, bank, done in ((0, 3 + q % 2, near_ready), (1, 5 + q % 2, far_ready)):
                    if q == 1 and what == 1 or q == 0 and what == 1:
                        pe.wait_ge(rel_copied, S // 8)
                    for k in range(K4):
                        for e in range(2):
                            blk = 2 * half + e
                            j0 = (S + WIN[blk], WIN[blk] + P)[what]
                            c0 = k * P + e * BLK
                            last = mm(ps[:, bank, c0:c0 + BLK], k_st[group(g), k, b, j0:j0 + P],
                                      q_st[group(g), k, b * S + blk * BLK:b * S + (blk + 1) * BLK],
                                      start=True, stop=True)
                    last.then_inc(done, 1)

            def values(q, b, half, g):
                pe.wait_ge(exp_near, q + 1)
                pe.wait_ge(exp_far, q + 1)
                if g == 0:
                    if q == 0:
                        pe.wait_ge(rel_copied, S // 8)
                    else:
                        pe.wait_ge(pv_copied, q // G)
                for k in range(K4):
                    h = K4 * g + k
                    o = ps[:, 7, h * 2 * VC:(h + 1) * 2 * VC]
                    mm(o, near[:, half * P:(half + 1) * P, b * H + h], vw[:, b, 2 * half:2 * half + 2, h, :],
                       start=True, stop=False)
                    last = mm(o, far[:, q % 2, k * P:(k + 1) * P],
                              vw[:, b, 4 + 2 * half:6 + 2 * half, h, :], start=False, stop=True)
                last.then_inc(pv_done, 1)
                if g == G - 1:
                    pass

            for half in range(2):
                for g in range(G):
                    natural(0, half, g)
            turn_maxima(0)
            before = None
            for q, b, half, g in units():
                scores(q, b, half, g)
                if b + 1 < B:
                    natural(b + 1, half, g)
                if before:
                    values(*before)
                before = (q, b, half, g)
                if q % 8 == 7 and b + 1 < B:
                    turn_maxima(b + 1)
            values(*before)

            for n in range(S // 2):
                blk = 2 * n // BLK
                o = 2 * n - WIN[blk]
                c0 = n % 32 * 2 * DK
                last = mm(ps[:, n // 32, c0:c0 + 2 * DK], near[:, 2 * n:2 * n + 2, :].rearrange("p i m -> p (i m)"),
                          rv[:, P - 2 - o:P - o, :].rearrange("p o d -> p (o d)"), start=True, stop=True)
                if n % 32 == 31:
                    last.then_inc(relv_ready, 1)

            pe.wait_ge(ld_late, 16 * N_LATE)
            pe.wait_ge(exp_far, 4 * 8)
            pe.wait_ge(pv_copied, 2 * B)
            for n in range(2):
                mm(ps[:, 6 + n, :], xw_sb[:, 1, :], ctx_sb[:, n * 512:(n + 1) * 512],
                   start=True, stop=True).then_inc(kT_ready, 1)

            pe.wait_ge(near_added, 4 * 8)
            pe.wait_ge(relv_even, 4)
            pe.wait_ge(relv_odd, 4)
            for half in range(2):
                for d in range(DK):
                    last = turn(ps[:, 4 + half, d * BH:(d + 1) * BH], rvo[:, half * P:(half + 1) * P, d],
                                con[0:BH, 0:BH])
                last.then_inc(relv_turned, 1)

            for n in range(2):
                for e in range(4):
                    t = 4 * n + e
                    last = mm(ps[:, 2 + n, e * D:(e + 1) * D], ctx_sb[:, t * P:(t + 1) * P], xw_sb[:, 2, :],
                              start=True, stop=True)
                last.then_inc(xv_ready, 1)

            pe.wait_ge(catt_done, 2)
            for n in range(2):
                for e in range(4):
                    t = 4 * n + e
                    last = turn(ps[:, n, e * P:(e + 1) * P],
                                catt[:, t % 2, t // 2 * H:(t // 2 + 1) * H, :].rearrange("p h d -> p (h d)"), ident)
                last.then_inc(cattT_ready, 1)
            for n in range(2):
                pe.wait_ge(cattT_copied, n + 1)
                for e in range(4):
                    t = 4 * n + e
                    last = mm(ps[:, 4 + n, e * D:(e + 1) * D], cattT[:, t * P:(t + 1) * P], wo_sb[:],
                              start=True, stop=True)
                last.then_inc(att_ready, 1)

            def turn_x(layer):
                if layer == 0:
                    pe.wait_ge(kT_copied, 2)
                for n in range(2):
                    pe.wait_ge(xn_done, NT * layer + 4 * n + 4)
                    for e in range(4):
                        t = 4 * n + e
                        last = turn(ps[:, 6 + n, e * P:(e + 1) * P], xn[:, layer, t, :], ident)
                    last.then_inc(xnT_ready, 1)

            turn_x(0)
            for n in range(2):
                pe.wait_ge(xnT_copied, n + 1)
                mm(ps[:, n, :], xw_sb[:, 0, :], xnT[:, 0, n * 512:(n + 1) * 512],
                   start=True, stop=True).then_inc(qT_ready, 1)
            pe.wait_ge(xv_copied, 2)
            for n in range(4):
                pe.wait_ge(qT_copied, n // 2 + 1)
                for e in range(2):
                    t = 2 * n + e
                    last = mm(ps[:, 2 + n, e * S:(e + 1) * S], qT[:, t * P:(t + 1) * P],
                              kT[:, n * S:(n + 1) * S], start=True, stop=True)
                last.then_inc(xs_ready, 1)
            for n in range(4):
                pe.wait_ge(xs_norm, 2 * n + 2)
                for e in range(4):
                    last = turn(ps[:, (6 + n) % 8, e * P:(e + 1) * P],
                                sc[:, 2 * n + e // 2, e % 2 * P:(e % 2 + 1) * P], ident)
                last.then_inc(pT_ready, 1)
            for b in range(B):
                pe.wait_ge(pT_copied, b + 1)
                for jh in range(2):
                    last = mm(ps[:, 2 + b // 2, b % 2 * S:(b % 2 + 1) * S], v_nat[:, 2 * b + jh, :],
                              pT[:, 2 * b:2 * b + 2, jh, :], start=(jh == 0), stop=(jh == 1))
                if b % 2:
                    last.then_inc(cT_ready, 1)
            for n in range(2):
                pe.wait_ge(cT_copied, n + 1)
                for e in range(4):
                    t = 4 * n + e
                    last = mm(ps[:, 4 + n, e * D:(e + 1) * D], cT[:, t * P:(t + 1) * P], xw_sb[:, 3, :],
                              start=True, stop=True)
                last.then_inc(att_ready, 1)
            turn_x(1)

            pe.wait_ge(ld_weights, 16 * N_WEIGHTS)
            for n in range(2 * NO):
                th, o = n // NO, n % NO
                if o == 0:
                    pe.wait_ge(xnT_copied, 3 + th)
                if n >= 2:
                    pe.wait_ge(gate_done, n - 1)
                bank = n % 2 * 2
                mm(ps[:, bank, :], w1_sb[:, o * P:(o + 1) * P], xnT[:, 1, th * 512:(th + 1) * 512],
                   start=True, stop=True)
                mm(ps[:, bank + 1, :], w2_sb[:, o * P:(o + 1) * P], xnT[:, 1, th * 512:(th + 1) * 512],
                   start=True, stop=True).then_inc(gate_ready, 1)
            for w, bank0, src, ready, given, free in (
                    (h1_sb, 4, 0, mid1_ready, gate_done, mid1_done), (h2_sb, 0, 1, mid2_ready, mid1_done, mid2_done)):
                for n in range(2 * NO):
                    th, o = n // NO, n % NO
                    pe.wait_ge(given, NO * (th + 1))
                    if src == 1 and n == 0:
                        pe.wait_ge(gate_done, 2 * NO)
                    if n >= 4:
                        pe.wait_ge(free, n - 3)
                    for k in range(NO):
                        last = mm(ps[:, bank0 + n % 4, :], w[:, k, o * P:(o + 1) * P],
                                  hid[:, src, k, th * 512:(th + 1) * 512], start=(k == 0), stop=(k == NO - 1))
                    last.then_inc(ready, 1)
            pe.wait_ge(mid1_done, 2 * NO)
            for n in range(2):
                pe.wait_ge(mid2_done, NO * (n + 1))
                for e in range(4):
                    t = 4 * n + e
                    for k in range(NO):
                        last = mm(ps[:, 4 + n, e * D:(e + 1) * D], hid[:, 2, k, t * P:(t + 1) * P],
                                  w3_sb[:, k, :], start=(k == 0), stop=(k == NO - 1))
                last.then_inc(ffn_ready, 1)

        @block.scalar
        def _(act):
            run = nc.scalar.activation

            act.wait_ge(ld_first, 16 * N_FIRST)
            for n in range(NJ):
                act.wait_ge(proj_ready, n + 1)
                if n >= 2:
                    act.wait_ge(split_done, n - 1)
                src = ps[:, n % QK_BANKS, :]
                run(raw[:, n % 2, :], src, ACT.Copy)
                if n % 2 == 0:
                    run(hi[:, 0, 0, :], src, ACT.Copy).then_inc(proj_read, 1)
                else:
                    run(hi[:, 1, 0, :], src, ACT.Identity, bias=relraw[:, 2 * P - 2:2 * P - 1])
                    run(hi[:, 1, 1, :], src, ACT.Identity, bias=relraw[:, 0:1]).then_inc(proj_read, 1)

            act.wait_ge(ones_set, 1)
            for b in range(B):
                act.wait_ge(v_ready, 2 * b + 1)
                run(vw[:, b, 0:4, :, 0:DK], ps[:, 4, :].rearrange("p (w h d) -> p w h d", w=4, h=H),
                    ACT.Copy).then_inc(v_copied[0], 1)

            for n in range(S // 8):
                act.wait_ge(rel_ready, n + 1)
                run(near[:, 8 * n:8 * n + 8, :].rearrange("p i m -> p (i m)"), ps[:, 6 + n % 2, :],
                    ACT.Copy).then_inc(rel_copied, 1)

            def copy_maxima(b):
                act.wait_ge(negm_turned, b + 1)
                run(mt[:, b, :], ps[0:2 * H, 2, 0:S], ACT.Copy).then_inc(negm_copied, 1)

            copy_maxima(0)
            for q, b, half, g in units():
                act.wait_ge(far_ready, q + 1)
                if q >= 2:
                    act.wait_ge(pv_done, q - 1)
                run(far[:, q % 2, :], ps[:, 5 + q % 2, :], ACT.Exp, scale=float(DK) ** -0.5).then_inc(exp_far, 1)
                act.wait_ge(near_added, q + 1)
                tile = near[:, half * P:(half + 1) * P, b * H + K4 * g:b * H + K4 * g + K4]
                run(tile, tile, ACT.Exp, scale=float(DK) ** -0.5).then_inc(exp_near, 1)
                if q % 8 == 7 and b + 1 < B:
                    copy_maxima(b + 1)

            for n in range(4):
                act.wait_ge(relv_ready, n + 1)
                run(rvo[:, BLK * n + 1:BLK * (n + 1):2, :],
                    ps[BH:P, n, :].rearrange("p (i e d) -> p i e d", e=2, d=DK)[:, :, 0, :],
                    ACT.Copy).then_inc(relv_odd, 1)
            for n in range(2):
                act.wait_ge(kT_ready, n + 1)
                run(kT[:, n * 512:(n + 1) * 512], ps[:, 6 + n, :], ACT.Identity, bias=cols[:, 1:2]).then_inc(kT_copied, 1)
            for n in range(2):
                act.wait_ge(cattT_ready, n + 1)
                run(cattT[:, n * 512:(n + 1) * 512], ps[:, n, :], ACT.Copy).then_inc(cattT_copied, 1)
            for n in range(2):
                act.wait_ge(xnT_ready, n + 1)
                run(xnT[:, 0, n * 512:(n + 1) * 512], ps[:, 6 + n, :], ACT.Copy).then_inc(xnT_copied, 1)
            for n in range(2):
                act.wait_ge(qT_ready, n + 1)
                run(qT[:, n * 512:(n + 1) * 512], ps[:, n, :], ACT.Identity, bias=cols[:, 0:1]).then_inc(qT_copied, 1)
            for t in range(NT):
                act.wait_ge(xs_max, t // 2 + 1)
                run(sc[:, t, :], sc[:, t, :], ACT.Exp, bias=smax[:, t:t + 1],
                    accum_out=ssum[:, t:t + 1]).then_inc(xs_exp, 1)
            for n in range(4):
                act.wait_ge(pT_ready, n + 1)
                run(pT[:, 2 * n:2 * n + 2, :, :].rearrange("p t j i -> p (t j i)"), ps[:, (6 + n) % 8, :],
                    ACT.Copy).then_inc(pT_copied, 1)
            for n in range(2):
                act.wait_ge(cT_ready, n + 1)
                run(cT[:, n * 512:(n + 1) * 512], ps[:, 2 + n, :], ACT.Copy).then_inc(cT_copied, 1)
            for n in range(2):
                act.wait_ge(xnT_ready, 3 + n)
                run(xnT[:, 1, n * 512:(n + 1) * 512], ps[:, 6 + n, :], ACT.Copy).then_inc(xnT_copied, 1)
            for n in range(2 * NO):
                act.wait_ge(gate_ready, n + 1)
                if n >= 2:
                    act.wait_ge(gate_done, n - 1)
                run(silu[:, n % 2, :], ps[:, n % 2 * 2, :], ACT.Silu,
                    scale=cols[:, 2 + n % NO:3 + n % NO]).then_inc(silu_done, 1)
            for bank0, dst, ready, done in ((4, 1, mid1_ready, mid1_done), (0, 2, mid2_ready, mid2_done)):
                for n in range(2 * NO):
                    th, o = n // NO, n % NO
                    act.wait_ge(ready, n + 1)
                    c0 = 2 + (1 + dst) * NO + o
                    run(hid[:, dst, o, th * 512:(th + 1) * 512], ps[:, bank0 + n % 4, :], ACT.Gelu,
                        scale=cols[:, c0:c0 + 1]).then_inc(done, 1)

        @block.gpsimd
        def _(pool):
            nc.gpsimd.memset(vw[:].rearrange("p b w h d -> p (b w h d)"), 1.0).then_inc(ones_set, 1)
            nc.gpsimd.memset(half_pow[:], -0.5).then_inc(pool_step, 1)
            pool.wait_ge(pool_step, 1)
            for layer in range(3):
                for n in range(2):
                    pool.wait_ge(ln_var, 2 * layer + n + 1)
                    r = rstd[:, layer, 4 * n:4 * n + 4]
                    nc.gpsimd.tensor_scalar(r, mv[:, layer, 4 * n:4 * n + 4, 1], EPS, None, ALU.add
                                            ).then_inc(pool_step, 1)
                    pool.wait_ge(pool_step, 2 + 2 * layer + n)
                    nc.gpsimd.tensor_tensor(r, r, half_pow[:, 4 * n:4 * n + 4], ALU.pow).then_inc(ln_rstd, 1)

        @block.vector
        def _(dve):
            v = nc.vector
            steps = [0]

            def settle(ins):
                steps[0] += 1
                ins.then_inc(dve_step, 1)
                dve.wait_ge(dve_step, steps[0])

            def col(c):
                return con[:, c:c + 1]

            dve.wait_ge(ld_first, 16 * N_FIRST)
            first, final = relraw[:, 0:1], relraw[:, 2 * P - 2:2 * P - 1]
            v.tensor_scalar(table_hi[:], relraw[:], first, None, ALU.subtract)
            v.tensor_scalar(table_t[:], relraw[:], first, col(KA), ALU.subtract, ALU.mult)
            v.tensor_scalar(kbias[:, 0:1], final, col(KA), col(KC), ALU.mult, ALU.add)
            settle(v.tensor_scalar(kbias[:, 1:2], first, col(KA), col(KC), ALU.mult, ALU.add))
            v.scalar_tensor_tensor(table[:], table_hi[:].bitcast(F32), col(KB), table_t[:],
                                   ALU.mult, ALU.add).then_inc(table_done, 1)

            for n in range(NJ):
                half, k = n // 8, n // 2 % 4
                dve.wait_ge(proj_read, n + 1)
                if n % 2 == 0:
                    settle(v.tensor_scalar(part[:, 0, 0, :], raw[:, 0, :], col(QA), None, ALU.mult))
                    v.scalar_tensor_tensor(q_st[:, k, half * 512:(half + 1) * 512], hi[:, 0, 0, :].bitcast(F32),
                                           col(QB), part[:, 0, 0, :], ALU.mult, ALU.add).then_inc(split_done, 1)
                else:
                    v.tensor_scalar(part[:, 1, 0, :], raw[:, 1, :], col(KA), kbias[:, 0:1], ALU.mult, ALU.add)
                    settle(v.tensor_scalar(part[:, 1, 1, :], raw[:, 1, :], col(KA), kbias[:, 1:2],
                                           ALU.mult, ALU.add))
                    for side in range(2):
                        last = v.scalar_tensor_tensor(
                            k_st[:, k, 2 * half:2 * half + 2, side * S:(side + 1) * S],
                            hi[:, 1, side, :].bitcast(F32).rearrange("p (b j) -> p b j", b=2), col(KB),
                            part[:, 1, side, :].rearrange("p (b j) -> p b j", b=2), ALU.mult, ALU.add)
                    last.then_inc(split_done, 1)

            dve.wait_ge(ones_set, 1)
            dve.wait_ge(ld_mid, 16 * N_MID)
            for b in range(B):
                dve.wait_ge(v_ready, 2 * b + 2)
                v.tensor_tensor(vw[:, b, 4:8, :, 0:DK], ps[:, 5, :].rearrange("p (w h d) -> p w h d", w=4, h=H),
                                rvfar[:].unsqueeze(2).to_broadcast([P, 4, H, DK]), ALU.add).then_inc(v_copied[1], 1)

            def maxima(b, half, g):
                u = (2 * b + half) * G + g
                for pair in range(2):
                    n, h = 2 * u + pair, K4 * g + 2 * pair
                    dve.wait_ge(nat_ready, n + 1)
                    v.tensor_reduce(mq[:, half, b, h:h + 2], ps[:, n % 2, :].rearrange("p (h j) -> p h j", h=2),
                                    AX.X, ALU.max).then_inc(nat_read, 1)
                dve.wait_ge(dist_ready, u + 1)
                v.tensor_reduce(mr[:, half, b, K4 * g:K4 * g + K4],
                                ps[:, 2, 0:K4 * 66].rearrange("p (h r) -> p h r", h=K4),
                                AX.X, ALU.max).then_inc(dist_read, 1)

            def shift(b):
                dve.wait_ge(dist_read, 8 * (b + 1))
                settle(v.scalar_tensor_tensor(negm[:, :, b, :], mq[:, :, b, :], -1.0, mr[:, :, b, :],
                                              ALU.mult, ALU.subtract))
                settle(v.tensor_copy(negm_hi[:, :, b, :], negm[:, :, b, :]))
                v.tensor_copy(negm_st[:, :, b, 0:H], negm_hi[:, :, b, :].bitcast(F32))
                settle(v.tensor_tensor(negm_st[:, :, b, H:2 * H], negm[:, :, b, :],
                                       negm_hi[:, :, b, :].bitcast(F32), ALU.subtract))
                dve.nop().then_inc(negm_done, 1)

            def add_relative(q, b, half, g):
                dve.wait_ge(near_ready, q + 1)
                if q == 0:
                    dve.wait_ge(rel_copied, S // 8)
                tile = near[:, half * P:(half + 1) * P, b * H + K4 * g:b * H + K4 * g + K4].rearrange("p i k -> p k i")
                v.tensor_tensor(tile, ps[:, 3 + q % 2, :].rearrange("p (k i) -> p k i", k=K4), tile,
                                ALU.add).then_inc(near_added, 1)

            def copy_values(q, b, half):
                dve.wait_ge(pv_done, q + 1)
                for e in range(2):
                    r = slice(e * BLK, (e + 1) * BLK)
                    last = v.tensor_copy(pvs[r, half, b * H:(b + 1) * H, :],
                                         ps[r, 7, 0:2 * VC * H].rearrange("p (h e d) -> p h e d", e=2, d=VC)[:, :, e, :])
                last.then_inc(pv_copied, 1)

            for half in range(2):
                for g in range(G):
                    maxima(0, half, g)
            shift(0)
            for q, b, half, g in units():
                if q % G == 0 and q:
                    pass
                add_relative(q, b, half, g)
                if b + 1 < B:
                    maxima(b + 1, half, g)
                if q % G == 1 and q > G:
                    copy_values(q - 2, (q - 2) // 8, (q - 2) // G % 2)
                if q % 8 == 7 and b + 1 < B:
                    shift(b + 1)
            copy_values(4 * 8 - 1, B - 1, 1)

            for n in range(4):
                dve.wait_ge(relv_ready, n + 1)
                v.tensor_copy(rvo[:, BLK * n:BLK * (n + 1):2, :],
                              ps[0:BH, n, :].rearrange("p (i e d) -> p i e d", e=2, d=DK)[:, :, 1, :]
                              ).then_inc(relv_even, 1)

            dve.wait_ge(pv_copied, 2 * B)
            settle(v.reciprocal(lsum[:], pvs[:, :, :, DK]))
            for half in range(2):
                dve.wait_ge(relv_turned, half + 1)
                settle(v.tensor_tensor(num[:, half], ps[:, 4 + half, :].rearrange("p (d m) -> p m d", d=DK),
                                       pvs[:, half, :, 0:DK], ALU.add))
                v.tensor_tensor(catt[:, half], num[:, half], lsum[:, half, :].unsqueeze(2).to_broadcast([P, BH, DK]),
                                ALU.mult).then_inc(catt_done, 1)

            dve.wait_ge(ld_late, 16 * N_LATE)
            dve.wait_ge(ld_weights, 16 * N_WEIGHTS)
            v.tensor_scalar(keep[:], mask_sb[:], 0.0, None, ALU.not_equal)
            v.tensor_scalar(pen[:], mask_sb[:], 0.0, NEG, ALU.is_equal, ALU.mult)
            for n in range(2):
                dve.wait_ge(xv_ready, n + 1)
                v.tensor_tensor(v_nat[:, 4 * n:4 * n + 4, :], ps[:, 2 + n, :].rearrange("p (t d) -> p t d", t=4),
                                rows[:, 1:2, :].to_broadcast([P, 4, D]), ALU.add).then_inc(xv_copied, 1)

            def residual(base, bias_row):
                settle(v.tensor_tensor(xb[:], base, rows[:, bias_row:bias_row + 1, :].to_broadcast([P, NT, D]),
                                       ALU.add))

            def norm(layer, ready, count, scale=None):
                for n in range(2):
                    dve.wait_ge(ready, count + n + 1)
                    t0 = slice(4 * n, 4 * n + 4)
                    src = ps[:, 4 + n, :].rearrange("p (t d) -> p t d", t=4)
                    if scale is not None:
                        settle(v.tensor_tensor(y[:, t0, :], src, scale, ALU.mult))
                        src = y[:, t0, :]
                    settle(v.tensor_tensor(y[:, t0, :], src, (xb if layer < 2 else xn[:, 1])[:, t0, :], ALU.add))
                    for t in range(4 * n, 4 * n + 4):
                        last = v.bn_stats(stats[:, t, :], y[:, t, :])
                    settle(last)
                    for t in range(4 * n, 4 * n + 4):
                        last = v.bn_aggr(mv[:, layer, t, :], stats[:, t, :])
                    last.then_inc(ln_var, 1)
                    dve.wait_ge(ln_rstd, 2 * layer + n + 1)
                    for t in range(4 * n, 4 * n + 4):
                        v.tensor_scalar(xn[:, layer, t, :], y[:, t, :], mv[:, layer, t, 0:1],
                                        rstd[:, layer, t:t + 1], ALU.subtract, ALU.mult).then_inc(xn_done, 1)

            residual(x_nat[:], 0)
            norm(0, att_ready, 0)
            dve.wait_ge(xn_done, NT)
            residual(xn[:, 0], 2)
            for n in range(4):
                dve.wait_ge(xs_ready, n + 1)
                two = slice(2 * n, 2 * n + 2)
                settle(v.scalar_tensor_tensor(sc[:, two, :], ps[:, 2 + n, :].rearrange("p (t j) -> p t j", t=2),
                                              float(D) ** -0.5, keep[:, two, :], ALU.mult, ALU.mult))
                settle(v.tensor_tensor(sc[:, two, :], sc[:, two, :], pen[:, two, :], ALU.add))
                v.tensor_reduce(smax[:, two], sc[:, two, :], AX.X, ALU.max, negate=True).then_inc(xs_max, 1)
            for t in range(NT):
                dve.wait_ge(xs_exp, t + 1)
                settle(v.reciprocal(srec[:, t:t + 1], ssum[:, t:t + 1]))
                v.tensor_scalar(sc[:, t, :], sc[:, t, :], srec[:, t:t + 1], None, ALU.mult).then_inc(xs_norm, 1)
            norm(1, att_ready, 2)

            for n in range(2 * NO):
                th, o = n // NO, n % NO
                dve.wait_ge(silu_done, n + 1)
                v.scalar_tensor_tensor(hid[:, 0, o, th * 512:(th + 1) * 512], ps[:, n % 2 * 2 + 1, :],
                                       cols[:, 2 + NO + o:3 + NO + o], silu[:, n % 2, :],
                                       ALU.mult, ALU.mult).then_inc(gate_done, 1)
            norm(2, ffn_ready, 0, rows[:, 3:4, :].to_broadcast([P, 4, D]))


def kernel(**inputs):
    import numpy as np
    import concourse.bacc as bacc
    from concourse.bass_utils import run_bass_kernel_spmd

    a = {k.replace("L0_", ""): np.asarray(v) for k, v in inputs.items()}
    tokens = a["x"].reshape(TOK, D)
    around = [j % S for j in range(HALO)]
    head_rows = [(K4 * g + k) * DK + d for k in range(K4) for g in range(G) for _ in range(4) for d in range(DK)]
    clipped = [min(max(u - (P - 1), -MAX_REL), MAX_REL) + MAX_REL for u in range(2 * P)]
    clipped[2 * P - 1] = clipped[2 * P - 2]
    far_rows = [[(0 if (w + P) + c >= S else NREL - 1) for w in WIN] for c in range(P)]
    consts = np.zeros((P, P + 8), np.float32)
    consts[:, :P] = np.eye(P, dtype=np.float32)
    for r in range(P):
        piece = r % 32 // DK
        consts[r, QA:KC + 1] = [(0, 0, 1, 0)[piece], (1, 1, -1, 0)[piece], (0, 1, 0, 0)[piece],
                                (1, -1, 1, 0)[piece], float(r % 32 in (24, 25))]

    def columns(s):
        return s.reshape(-1, P).T

    arrays = dict(
        x=tokens, xT=a["x"].transpose(2, 0, 1)[:, :, around],
        ctxT=a["ctx_1024"].reshape(TOK, D).T, mask=a["mask_BxSxS2_if1"].reshape(TOK, S),
        consts=consts,
        wqr=a["attn_Wq"].T[:, head_rows].reshape(D, K4, P), wkr=a["attn_Wk"].T[:, head_rows].reshape(D, K4, P),
        wvT=a["attn_Wv"].T, woT=a["attn_Wo"].T, b_o=a["attn_b_o"],
        relk=np.tile(a["attn_rel_k_emb"][clipped].T, (16, 1)),
        relv=a["attn_rel_v_emb"][clipped], relv_far=a["attn_rel_v_emb"][far_rows],
        xwq=a["xattn_Wq"].T, xbq=a["xattn_bq"].reshape(D, 1), xwk=a["xattn_Wk"].T, xbk=a["xattn_bk"].reshape(D, 1),
        xwv=a["xattn_Wv"].T, xbv=a["xattn_bv"], xwo=a["xattn_Wo"].T, xbo=a["xattn_bo"],
        w1=a["ffn_w1_w"].T, s1=columns(a["ffn_w1_s"]), w2=a["ffn_w2_w"].T, s2=columns(a["ffn_w2_s"]),
        h1=a["ffn_h1_w"].T, hs=np.concatenate([columns(a["ffn_h1_s"]), columns(a["ffn_h2_s"])], 1),
        h2=a["ffn_h2_w"].T, w3=a["ffn_w3_w"].T, s3=a["ffn_w3_s"])
    arrays = {k: np.ascontiguousarray(v) for k, v in arrays.items()}

    nc = bacc.Bacc("TRN2", target_bir_lowering=False, num_devices=1)
    ap = {k: nc.dram_tensor("in_" + k, v.shape, mybir.dt.from_np(v.dtype), kind="ExternalInput").ap()
          for k, v in arrays.items()}
    result = nc.dram_tensor("out", (TOK, D), F32, kind="ExternalOutput").ap()
    build(nc, *(ap.get(n) for n in (
        "x", "xT", "ctxT", "mask", "consts", "wqr", "wkr", "wvT", "woT", "b_o", "relk", "relv", "relv_far",
        "xwq", "xbq", "xwk", "xbk", "xwv", "xbv", "xwo", "xbo",
        "w1", "s1", "w2", "s2", "h1", "hs", "h2", "w3", "s3")), result)
    r = run_bass_kernel_spmd(nc, [{"in_" + k: v for k, v in arrays.items()}], core_ids=[0])
    return r.results[0]["out"].reshape(B, S, D)
```

```python
from contextlib import ExitStack

import concourse.bass as bass
from concourse import mybir

F32 = mybir.dt.float32
BF16 = mybir.dt.bfloat16
I32 = mybir.dt.int32
ALU = mybir.AluOpType
ACT = mybir.ActivationFunctionType
AX = mybir.AxisListType

P = 128
B, S, D = 4, 256, 128
H, DK = 16, 8
G, K4 = 4, 4
PAIRS = H // 2
STACK = [(0, 0), (0, 1), (0, 2), (1, 0), (1, 1), (2, 0)]
SHIFT = len(STACK) * DK
WIDE = 128
TOK = B * S
NT = TOK // P
HID = 512
NO = HID // P
MAX_REL = 32
NREL = 2 * MAX_REL + 1
BLK = 64
WIN = [0, 32, 96, 128]
VWIN = WIN + [(w + P) % S for w in WIN]
EPS = 1e-5
NEG = -1.0e9
HALO = 384
BH = B * H
VC = DK + 1

HI, MID, LO = range(P, P + 3)


def build(nc, x, xT, ctxT, mask, consts, ones, wqT, wkT, wvT, woT, b_o, relk, relv, relv_far,
          xwq, xbq, xwk, xbk, xwv, xbv, xwo, xbo,
          w1, s1, w2, s2, h1, hs, h2, w3, s3, out):
    with ExitStack() as ctx:
        def sb(name, shape, dt=F32, stack=ctx):
            return stack.enter_context(nc.sbuf_tensor(name, shape, dt))

        def sem(name):
            return ctx.enter_context(nc.semaphore(name))

        ps = ctx.enter_context(nc.psum_tensor("ps", [P, 8, 512], F32))

        con = sb("con", [P, P + 8])
        ident = con[:, 0:P]
        x_nat = sb("x_nat", [P, NT, D])
        ctx_sb = sb("ctx_sb", [P, TOK])
        wo_sb = sb("wo_sb", [P, D])
        xw_sb = sb("xw_sb", [P, 4, D])
        rows = sb("rows", [P, 4, D])
        cols = sb("cols", [P, 2 + 4 * NO])
        near = sb("near", [P, S, BH])
        rv = sb("rv", [P, P * DK + WIDE - 2 * DK])
        pvs = sb("pvs", [P, 2, BH, VC])
        half_pow = sb("half_pow", [P, NT])
        mv = sb("mv", [P, 3, NT, 2])
        rstd = sb("rstd", [P, 3, NT])
        stats = sb("stats", [P, NT, 6])

        early = ExitStack()
        xT_sb = sb("xT_sb", [P, B, HALO], stack=early)
        wv_sb = sb("wv_sb", [P, D], stack=early)
        table = sb("table", [P, 2 * P], BF16, stack=early)
        rvfar = sb("rvfar", [P, 4, DK], stack=early)
        q_st = sb("q_st", [P, PAIRS, 2, B, S], BF16, stack=early)
        k_st = sb("k_st", [P, PAIRS, B, 2 * S], BF16, stack=early)
        V_RUN = 2 * B * 2 * H * 2 * VC
        vw = sb("vw", [P, V_RUN + WIDE - 2 * VC], stack=early)
        vw_at = vw[:, 0:V_RUN].rearrange("p (b s f h e d) -> p b s f h e d", b=B, s=2, f=2, h=H, e=2)
        mq = sb("mq", [P, 2, B, H], stack=early)
        mr = sb("mr", [P, 2, B, H], stack=early)
        negm = sb("negm", [P, 2, B, H], stack=early)
        negm_left = sb("negm_left", [P, 2, B, H], stack=early)
        negm_bf = sb("negm_bf", [P, 2, 2, B, H], BF16, stack=early)
        negm_st = sb("negm_st", [P, 2, B, 3 * H], stack=early)
        mt = sb("mt", [3 * H, B, S], BF16, stack=early)
        with ExitStack() as projecting:
            wq_sb = sb("wq_sb", [P, D], stack=projecting)
            wk_sb = sb("wk_sb", [P, D], stack=projecting)
            relraw = sb("relraw", [P, 2 * P], stack=projecting)
            cut_bf = sb("cut_bf", [P, 2, 2 * P], BF16, stack=projecting)
            q_part = sb("q_part", [P, 2, 3, 512], BF16, stack=projecting)
            k_part = sb("k_part", [P, 2, 3, 2, 2, S], BF16, stack=projecting)
        far = sb("far", [P, 2, 512], stack=early)
        early.close()

        mask_sb = sb("mask_sb", [P, NT, S], I32)
        w1_sb = sb("w1_sb", [P, HID])
        w2_sb = sb("w2_sb", [P, HID])
        h1_sb = sb("h1_sb", [P, NO, HID])
        h2_sb = sb("h2_sb", [P, NO, HID])
        w3_sb = sb("w3_sb", [P, NO, D])
        rvo = sb("rvo", [BH, S, DK])
        lsum = sb("lsum", [P, 2, BH])
        num = sb("num", [P, 2, BH, DK])
        catt = sb("catt", [P, 2, BH, DK])
        cattT = sb("cattT", [P, TOK])
        y = sb("y", [P, NT, D])
        xb = sb("xb", [P, NT, D])
        xn = sb("xn", [P, 3, NT, D])
        xnT = sb("xnT", [P, 2, TOK])
        qT = sb("qT", [P, TOK])
        kT = sb("kT", [P, TOK])
        v_nat = sb("v_nat", [P, NT, D])
        keep = sb("keep", [P, NT, S])
        pen = sb("pen", [P, NT, S])
        sc = sb("sc", [P, NT, S])
        smax = sb("smax", [P, NT])
        ssum = sb("ssum", [P, NT])
        srec = sb("srec", [P, NT])
        silu = sb("silu", [P, 2, 512])
        flat = near[:, :, :].rearrange("p i m -> p (i m)")
        full, left = (flat[:, n * 3072:(n + 1) * 3072].rearrange("p (f w t) -> p f w t", f=2, w=3) for n in range(2))
        cut = flat[:, 2 * 3072:2 * 3072 + 5 * 2 * P].rearrange("p (n u) -> p n u", n=5)
        hid = flat[:, 0:3 * NO * TOK].rearrange("p (l o t) -> p l o t", l=3, o=NO)
        rest = 3 * NO * TOK
        pT = flat[:, rest:rest + 2 * TOK].rearrange("p (t j i) -> p t j i", t=NT, j=2)
        cT = flat[:, rest + 2 * TOK:rest + 3 * TOK]

        q_way = nc.dram_tensor("q_way", [len(STACK), D, TOK], BF16, kind="Internal").ap()
        k_way = nc.dram_tensor("k_way", [len(STACK), D, 2 * TOK], BF16, kind="Internal").ap()
        m_way = nc.dram_tensor("m_way", [B, 3, 2, PAIRS, S], BF16, kind="Internal").ap()

        ld_first, ld_mid, ld_late = sem("ld_first"), sem("ld_mid"), sem("ld_late")
        ld_weights = sem("ld_weights")
        proj_ready, full_done, parts_done = sem("proj_ready"), sem("full_done"), sem("parts_done")
        ones_placed, zeros_set = sem("ones_placed"), sem("zeros_set")
        parts_out = [sem(f"parts_out{n}") for n in range(2)]
        stacked = [sem(f"stacked{n}") for n in range(2)]
        dve_step = sem("dve_step")
        ones_set, v_ready = sem("ones_set"), sem("v_ready")
        v_copied = [sem("v_copied_win"), sem("v_copied_far")]
        table_done = sem("table_done")
        rel_ready, rel_copied = sem("rel_ready"), sem("rel_copied")
        nat_ready, nat_read = sem("nat_ready"), sem("nat_read")
        dist_ready, dist_read = sem("dist_ready"), sem("dist_read")
        negm_done, negm_turned, negm_copied = sem("negm_done"), sem("negm_turned"), sem("negm_copied")
        shift_out = [sem(f"shift_out{b}") for b in range(B)]
        shift_placed = [sem(f"shift_placed{b}") for b in range(B)]
        near_ready, far_ready, near_added = sem("near_ready"), sem("far_ready"), sem("near_added")
        exp_near, exp_far = sem("exp_near"), sem("exp_far")
        pv_done, pv_ready, pv_copied = sem("pv_done"), sem("pv_ready"), sem("pv_copied")
        relv_ready, relv_even, relv_odd = sem("relv_ready"), sem("relv_even"), sem("relv_odd")
        relv_turned, catt_done = sem("relv_turned"), sem("catt_done")
        cattT_ready, cattT_copied = sem("cattT_ready"), sem("cattT_copied")
        kT_ready, kT_copied = sem("kT_ready"), sem("kT_copied")
        xv_ready, xv_copied = sem("xv_ready"), sem("xv_copied")
        att_ready, ln_var, ln_rstd = sem("att_ready"), sem("ln_var"), sem("ln_rstd")
        y_done, pool_step = sem("y_done"), sem("pool_step")
        xn_done, xnT_ready, xnT_copied = sem("xn_done"), sem("xnT_ready"), sem("xnT_copied")
        qT_ready, qT_copied = sem("qT_ready"), sem("qT_copied")
        xs_ready, xs_max, xs_exp, xs_norm = sem("xs_ready"), sem("xs_max"), sem("xs_exp"), sem("xs_norm")
        xs_masked = sem("xs_masked")
        pT_ready, pT_copied = sem("pT_ready"), sem("pT_copied")
        cT_ready, cT_copied = sem("cT_ready"), sem("cT_copied")
        gate_ready, silu_done, gate_done = sem("gate_ready"), sem("silu_done"), sem("gate_done")
        mid1_ready, mid1_done = sem("mid1_ready"), sem("mid1_done")
        mid2_ready, mid2_done = sem("mid2_ready"), sem("mid2_done")
        ffn_ready, stored = sem("ffn_ready"), sem("stored")

        N_FIRST, N_MID, N_LATE, N_WEIGHTS = 5, 5, 14, 6
        Q_WAYS = 6

        def heads_of(near, b, half, g):
            return near[:, half * P:(half + 1) * P, :].rearrange("p i (h b) -> p b h i", b=B)[
                :, b, K4 * g:K4 * g + K4, :]

        def units():
            for q in range(B * 2 * G):
                yield q, q // 8, q // G % 2, q % G

        block = ctx.enter_context(nc.Block())

        @block.sync
        def _(sp):
            for dst, src in ((xT_sb, xT), (wq_sb, wqT), (wk_sb, wkT), (con, consts), (relraw, relk)):
                sp.dma_start(dst[:], src).then_inc(ld_first, 16)
            for side in range(2):
                r = side * BLK + SHIFT
                sp.dma_start(k_st[r:(side + 1) * BLK].rearrange("p a b j -> p (a b j)"),
                             ones.partition_broadcast(BLK - SHIFT)).then_inc(ones_placed, 16)
            for dst, src in ((wv_sb[:], wvT), (wo_sb[:], woT),
                             (x_nat[:], x.rearrange("(t p) d -> p t d", p=P)), (rvfar[:], relv_far)):
                sp.dma_start(dst, src).then_inc(ld_mid, 16)
            slide = bass.AP(relv.tensor, 0, [[DK, P], [1, P * DK + WIDE - 2 * DK]])
            sp.dma_start(rv[:], slide).then_inc(ld_mid, 16)

            for half in range(2):
                sp.wait_ge(parts_done, 3 * (half + 1))
                for p, (qp, kp) in enumerate(STACK):
                    sp.dma_start(q_way[p, :, half * 512:(half + 1) * 512],
                                 q_part[:, half, qp, :]).then_inc(parts_out[half], 16)
                    sp.dma_start(k_way[p, :, half * 1024:(half + 1) * 1024],
                                 k_part[:, half, kp].rearrange("p b s j -> p (b s j)")).then_inc(parts_out[half], 16)
                if half == 0:
                    sp.wait_ge(zeros_set, 1)
                sp.wait_ge(parts_out[half], 16 * 2 * Q_WAYS)
                for e in range(2):
                    for p in range(len(STACK)):
                        r = slice(e * BLK + p * DK, e * BLK + (p + 1) * DK)
                        sp.dma_start(q_st[r, :, e, 2 * half:2 * half + 2, :].rearrange("p a b i -> p a (b i)"),
                                     q_way[p].rearrange("(a e d) t -> e d a t", e=2, d=DK)
                                     [e, :, :, half * 512:(half + 1) * 512]).then_inc(stacked[half], 16)
                        sp.dma_start(k_st[r, :, 2 * half:2 * half + 2, :].rearrange("p a b i -> p a (b i)"),
                                     k_way[p].rearrange("(a e d) t -> e d a t", e=2, d=DK)
                                     [e, :, :, half * 1024:(half + 1) * 1024]).then_inc(stacked[half], 16)

            late = ((ctx_sb[:], ctxT), (xw_sb[:, 0, :], xwq), (xw_sb[:, 1, :], xwk), (xw_sb[:, 2, :], xwv),
                    (xw_sb[:, 3, :], xwo),
                    (rows[:, 0, :], b_o.partition_broadcast(P)), (rows[:, 1, :], xbv.partition_broadcast(P)),
                    (rows[:, 2, :], xbo.partition_broadcast(P)), (rows[:, 3, :], s3.partition_broadcast(P)),
                    (cols[:, 0:1], xbq), (cols[:, 1:2], xbk),
                    (cols[:, 2:2 + NO], s1), (cols[:, 2 + NO:2 + 2 * NO], s2),
                    (cols[:, 2 + 2 * NO:2 + 4 * NO], hs))
            for dst, src in late:
                sp.dma_start(dst, src).then_inc(ld_late, 16)

            for b in range(B):
                sp.wait_ge(negm_copied, b + 1)
                sp.dma_start(m_way[b].rearrange("m e a i -> (m e a) i"), mt[:, b, :]).then_inc(shift_out[b], 16)
                sp.wait_ge(shift_out[b], 16)
                if b == 0:
                    sp.wait_ge(rel_ready, S // 8)
                for e in range(2):
                    r = e * BLK + SHIFT
                    sp.dma_start(q_st[r:r + 3, :, e, b, :], m_way[b, :, e]).then_inc(shift_placed[b], 16)

            sp.wait_ge(pv_done, 4 * 8)
            for dst, src in ((mask_sb[:], mask.rearrange("(t p) j -> p t j", p=P)), (w1_sb[:], w1), (w2_sb[:], w2),
                             (h1_sb[:], h1.rearrange("(k p) o -> p k o", p=P)),
                             (h2_sb[:], h2.rearrange("(k p) o -> p k o", p=P)),
                             (w3_sb[:], w3.rearrange("(k p) o -> p k o", p=P))):
                sp.dma_start(dst, src).then_inc(ld_weights, 16)

            sp.wait_ge(xn_done, 3 * NT)
            sp.dma_start(out.rearrange("(t p) d -> p t d", p=P), xn[:, 2]).then_inc(stored, 16)
            sp.wait_ge(stored, 16)

        @block.tensor
        def _(pe):
            mm, turn = nc.tensor.matmul, nc.tensor.transpose

            pe.wait_ge(ld_first, 16 * N_FIRST)
            for n in range(4):
                mm(ps[:, n, :], (wq_sb, wk_sb)[n % 2][:], xT_sb[:, n // 2 * 2:n // 2 * 2 + 2, 0:S],
                   start=True, stop=True).then_inc(proj_ready, 1)

            pe.wait_ge(ld_mid, 16 * N_MID)
            for n in range(2 * B):
                b, side = n // 2, n % 2
                if n >= 2:
                    pe.wait_ge(v_copied[side], n // 2)
                for w in range(4):
                    j0 = VWIN[4 * side + w]
                    last = mm(ps[:, 4 + n % 2, w * D:(w + 1) * D], xT_sb[:, b, j0:j0 + P], wv_sb[:],
                              start=True, stop=True)
                last.then_inc(v_ready, 1)

            def relative(n):
                if n >= 2:
                    pe.wait_ge(rel_copied, n - 1)
                for e in range(8):
                    i = 8 * n + e
                    o = i - WIN[i // BLK]
                    last = mm(ps[:, 6 + n % 2, e * BH:(e + 1) * BH], table[:, P - 1 - o:2 * P - 1 - o],
                              q_st[:, :, :, :, i].rearrange("p a e b -> p (a e b)"), start=True, stop=True)
                last.then_inc(rel_ready, 1)

            def natural(b, half, g):
                u = (2 * b + half) * G + g
                for pair in range(2):
                    n = 2 * u + pair
                    if n >= 2:
                        pe.wait_ge(nat_read, n - 1)
                    for e in range(2):
                        last = mm(ps[:, n % 2, e * S:(e + 1) * S],
                                  q_st[:, 2 * g + pair, e, b, half * P:(half + 1) * P],
                                  k_st[:, 2 * g + pair, b, S:2 * S], start=True, stop=True)
                    last.then_inc(nat_ready, 1)
                if u >= 1:
                    pe.wait_ge(dist_read, u)
                if half == 0 and g == 0 and b >= 1:
                    pe.wait_ge(negm_copied, b)
                for k in range(K4):
                    last = mm(ps[:, 2, k * 66:k * 66 + 66],
                              q_st[:, 2 * g + k // 2, k % 2, b, half * P:(half + 1) * P],
                              table[:, P - 1 - MAX_REL:P - 1 - MAX_REL + 66], start=True, stop=True)
                last.then_inc(dist_ready, 1)

            def turn_maxima(b):
                pe.wait_ge(negm_done, b + 1)
                for half in range(2):
                    last = turn(ps[0:3 * H, 2, half * P:(half + 1) * P], negm_st[:, half, b, :], ident)
                last.then_inc(negm_turned, 1)

            def scores(q, b, half, g):
                if q == 0:
                    pe.wait_ge(v_copied[0], B)
                    pe.wait_ge(v_copied[1], B)
                if q % 8 == 0:
                    pe.wait_ge(shift_placed[b], 16 * 2)
                if q >= 2:
                    pe.wait_ge(near_added, q - 1)
                    pe.wait_ge(exp_far, q - 1)
                for what, bank, done in ((0, 3 + q % 2, near_ready), (1, 5 + q % 2, far_ready)):
                    if q < 2 and what == 1:
                        pe.wait_ge(rel_copied, S // 8)
                    for pair in range(2):
                        for e in range(2):
                            blk = 2 * half + e
                            j0 = (S + WIN[blk], WIN[blk] + P)[what]
                            o = ps[:, bank, pair * S:(pair + 1) * S].rearrange(
                                "p (k f i) -> p k f i", k=2, f=2)[:, :, e, :]
                            last = mm(o, k_st[:, 2 * g + pair, b, j0:j0 + P],
                                      q_st[:, 2 * g + pair, :, b, blk * BLK:(blk + 1) * BLK],
                                      start=True, stop=True)
                    last.then_inc(done, 1)

            def vw_run(b, side, half, h):
                at = (((b * 2 + side) * 2 + half) * H + h) * 2 * VC
                return vw[:, at:at + WIDE]

            def values(q, b, half, g):
                pe.wait_ge(exp_near, q + 1)
                pe.wait_ge(exp_far, q + 1)
                if g == 0:
                    if q == 0:
                        pe.wait_ge(rel_copied, S // 8)
                    else:
                        pe.wait_ge(pv_copied, q // G)
                for k in range(K4):
                    h = K4 * g + k
                    o = ps[:, 7, h * 2 * VC:h * 2 * VC + WIDE]
                    mm(o, near[:, half * P:(half + 1) * P, h * B + b], vw_run(b, 0, half, h),
                       start=True, stop=False)
                    last = mm(o, far[:, q % 2, k * P:(k + 1) * P], vw_run(b, 1, half, h),
                              start=False, stop=True)
                last.then_inc(pv_done, 1)

            pe.wait_ge(full_done, 6)
            pe.wait_ge(stacked[0], 16 * 4 * len(STACK))
            pe.wait_ge(ones_placed, 16 * 2)
            pe.wait_ge(table_done, 1)
            for u in range(2 * G):
                natural(0, u // G, u % G)
            turn_maxima(0)
            for u in range(2):
                natural(1, 0, u)
            pe.wait_ge(stacked[1], 16 * 4 * len(STACK))
            for n in range(S // 8):
                relative(n)
                if n % 8 == 7 and n < 24:
                    u = 2 + n // 8
                    natural(1, u // G, u % G)
            for u in range(5, 2 * G):
                natural(1, u // G, u % G)
            before = None
            for q, b, half, g in units():
                scores(q, b, half, g)
                if q % 8 == 0 and b + 1 < B:
                    turn_maxima(b + 1)
                if b + 2 < B:
                    natural(b + 2, half, g)
                if before:
                    values(*before)
                before = (q, b, half, g)
            values(*before)

            for n in range(S // 2):
                job, o = n // 16, 2 * n - WIN[2 * n // BLK]
                if n % 16 == 0 and job >= 4:
                    pe.wait_ge(relv_even, job - 3)
                    pe.wait_ge(relv_odd, job - 3)
                c0, r0 = n % 16 * 2 * DK, (P - 2 - o) * DK
                last = mm(ps[:, job % 4, c0:c0 + WIDE], near[:, 2 * n:2 * n + 2, :].rearrange("p i m -> p (i m)"),
                          rv[:, r0:r0 + WIDE], start=True, stop=True)
                if n % 16 == 15:
                    last.then_inc(relv_ready, 1)

            pe.wait_ge(ld_late, 16 * N_LATE)
            pe.wait_ge(exp_far, 4 * 8)
            pe.wait_ge(pv_copied, 2 * B)
            for n in range(2):
                mm(ps[:, 6 + n, :], xw_sb[:, 1, :], ctx_sb[:, n * 512:(n + 1) * 512],
                   start=True, stop=True).then_inc(kT_ready, 1)

            pe.wait_ge(near_added, 4 * 8)
            pe.wait_ge(relv_even, 8)
            pe.wait_ge(relv_odd, 8)
            for half in range(2):
                for d in range(DK):
                    last = turn(ps[:, 4 + half, d * BH:(d + 1) * BH], rvo[:, half * P:(half + 1) * P, d],
                                con[0:BH, 0:BH])
                last.then_inc(relv_turned, 1)

            for n in range(2):
                for e in range(4):
                    t = 4 * n + e
                    last = mm(ps[:, 2 + n, e * D:(e + 1) * D], ctx_sb[:, t * P:(t + 1) * P], xw_sb[:, 2, :],
                              start=True, stop=True)
                last.then_inc(xv_ready, 1)

            pe.wait_ge(catt_done, 2)
            for n in range(2):
                for e in range(4):
                    t = 4 * n + e
                    last = turn(ps[:, n, e * P:(e + 1) * P],
                                catt[:, t % 2, t // 2 * H:(t // 2 + 1) * H, :].rearrange("p h d -> p (h d)"), ident)
                last.then_inc(cattT_ready, 1)
            for n in range(2):
                pe.wait_ge(cattT_copied, n + 1)
                for e in range(4):
                    t = 4 * n + e
                    last = mm(ps[:, 4 + n, e * D:(e + 1) * D], cattT[:, t * P:(t + 1) * P], wo_sb[:],
                              start=True, stop=True)
                last.then_inc(att_ready, 1)

            def turn_x(layer):
                if layer == 0:
                    pe.wait_ge(kT_copied, 2)
                for n in range(2):
                    pe.wait_ge(xn_done, NT * layer + 4 * n + 4)
                    for e in range(4):
                        t = 4 * n + e
                        last = turn(ps[:, 6 + n, e * P:(e + 1) * P], xn[:, layer, t, :], ident)
                    last.then_inc(xnT_ready, 1)

            turn_x(0)
            for n in range(2):
                pe.wait_ge(xnT_copied, n + 1)
                mm(ps[:, n, :], xw_sb[:, 0, :], xnT[:, 0, n * 512:(n + 1) * 512],
                   start=True, stop=True).then_inc(qT_ready, 1)
            pe.wait_ge(xv_copied, 2)
            for n in range(4):
                pe.wait_ge(qT_copied, n // 2 + 1)
                for e in range(2):
                    t = 2 * n + e
                    last = mm(ps[:, 2 + n, e * S:(e + 1) * S], qT[:, t * P:(t + 1) * P],
                              kT[:, n * S:(n + 1) * S], start=True, stop=True)
                last.then_inc(xs_ready, 1)
            for n in range(4):
                pe.wait_ge(xs_norm, 2 * n + 2)
                for e in range(4):
                    last = turn(ps[:, (6 + n) % 8, e * P:(e + 1) * P],
                                sc[:, 2 * n + e // 2, e % 2 * P:(e % 2 + 1) * P], ident)
                last.then_inc(pT_ready, 1)
            for b in range(B):
                pe.wait_ge(pT_copied, b + 1)
                for jh in range(2):
                    last = mm(ps[:, 2 + b // 2, b % 2 * S:(b % 2 + 1) * S], v_nat[:, 2 * b + jh, :],
                              pT[:, 2 * b:2 * b + 2, jh, :], start=(jh == 0), stop=(jh == 1))
                if b % 2:
                    last.then_inc(cT_ready, 1)
            for n in range(2):
                pe.wait_ge(cT_copied, n + 1)
                for e in range(4):
                    t = 4 * n + e
                    last = mm(ps[:, 4 + n, e * D:(e + 1) * D], cT[:, t * P:(t + 1) * P], xw_sb[:, 3, :],
                              start=True, stop=True)
                last.then_inc(att_ready, 1)
            turn_x(1)

            pe.wait_ge(ld_weights, 16 * N_WEIGHTS)
            for n in range(2 * NO):
                th, o = n // NO, n % NO
                if o == 0:
                    pe.wait_ge(xnT_copied, 3 + th)
                if n >= 2:
                    pe.wait_ge(gate_done, n - 1)
                bank = n % 2 * 2
                mm(ps[:, bank, :], w1_sb[:, o * P:(o + 1) * P], xnT[:, 1, th * 512:(th + 1) * 512],
                   start=True, stop=True)
                mm(ps[:, bank + 1, :], w2_sb[:, o * P:(o + 1) * P], xnT[:, 1, th * 512:(th + 1) * 512],
                   start=True, stop=True).then_inc(gate_ready, 1)
            for w, bank0, src, ready, given, free in (
                    (h1_sb, 4, 0, mid1_ready, gate_done, mid1_done), (h2_sb, 0, 1, mid2_ready, mid1_done, mid2_done)):
                for n in range(2 * NO):
                    th, o = n // NO, n % NO
                    pe.wait_ge(given, NO * (th + 1))
                    if src == 1 and n == 0:
                        pe.wait_ge(gate_done, 2 * NO)
                    if n >= 4:
                        pe.wait_ge(free, n - 3)
                    for k in range(NO):
                        last = mm(ps[:, bank0 + n % 4, :], w[:, k, o * P:(o + 1) * P],
                                  hid[:, src, k, th * 512:(th + 1) * 512], start=(k == 0), stop=(k == NO - 1))
                    last.then_inc(ready, 1)
            pe.wait_ge(mid1_done, 2 * NO)
            for n in range(2):
                pe.wait_ge(mid2_done, NO * (n + 1))
                for e in range(4):
                    t = 4 * n + e
                    for k in range(NO):
                        last = mm(ps[:, 4 + n, e * D:(e + 1) * D], hid[:, 2, k, t * P:(t + 1) * P],
                                  w3_sb[:, k, :], start=(k == 0), stop=(k == NO - 1))
                last.then_inc(ffn_ready, 1)

        @block.scalar
        def _(act):
            run = nc.scalar.activation

            act.wait_ge(ld_first, 16 * N_FIRST)
            first, final = relraw[:, 0:1], relraw[:, 2 * P - 2:2 * P - 1]
            for half in range(2):
                act.wait_ge(proj_ready, 2 * half + 1)
                run(full[:, half, 0, :], ps[:, 2 * half, :], ACT.Copy).then_inc(full_done, 1)
                act.wait_ge(proj_ready, 2 * half + 2)
                for side, bias in ((0, final), (1, first)):
                    run(full[:, half, 1 + side, :], ps[:, 2 * half + 1, :], ACT.Identity,
                        bias=bias).then_inc(full_done, 1)

            act.wait_ge(ones_set, 1)
            for b in range(B):
                act.wait_ge(v_ready, 2 * b + 1)
                for half in range(2):
                    last = run(vw_at[:, b, 0, half, :, :, 0:DK].rearrange("p h e d -> p e h d"),
                               ps[:, 4, half * S:(half + 1) * S].rearrange("p (e h d) -> p e h d", e=2, h=H), ACT.Copy)
                last.then_inc(v_copied[0], 1)

            def copy_maxima(b):
                act.wait_ge(negm_turned, b + 1)
                run(mt[:, b, :], ps[0:3 * H, 2, 0:S], ACT.Copy).then_inc(negm_copied, 1)

            copy_maxima(0)
            for n in range(S // 8):
                act.wait_ge(rel_ready, n + 1)
                run(near[:, 8 * n:8 * n + 8, :].rearrange("p i m -> p (i m)"), ps[:, 6 + n % 2, :],
                    ACT.Copy).then_inc(rel_copied, 1)

            for q, b, half, g in units():
                act.wait_ge(far_ready, q + 1)
                if q >= 2:
                    act.wait_ge(pv_done, q - 1)
                run(far[:, q % 2, :], ps[:, 5 + q % 2, :], ACT.Exp, scale=float(DK) ** -0.5).then_inc(exp_far, 1)
                if q % 8 == 0 and b + 1 < B:
                    copy_maxima(b + 1)
                act.wait_ge(near_added, q + 1)
                tile = heads_of(near, b, half, g)
                run(tile, tile, ACT.Exp, scale=float(DK) ** -0.5).then_inc(exp_near, 1)

            for n in range(8):
                act.wait_ge(relv_ready, n + 1)
                run(rvo[:, 32 * n + 1:32 * (n + 1):2, :],
                    ps[BH:P, n % 4, 0:32 * DK].rearrange("p (i e d) -> p i e d", e=2, d=DK)[:, :, 0, :],
                    ACT.Copy).then_inc(relv_odd, 1)
            for n in range(2):
                act.wait_ge(kT_ready, n + 1)
                run(kT[:, n * 512:(n + 1) * 512], ps[:, 6 + n, :], ACT.Identity, bias=cols[:, 1:2]).then_inc(kT_copied, 1)
            for n in range(2):
                act.wait_ge(cattT_ready, n + 1)
                run(cattT[:, n * 512:(n + 1) * 512], ps[:, n, :], ACT.Copy).then_inc(cattT_copied, 1)
            for n in range(2):
                act.wait_ge(xnT_ready, n + 1)
                run(xnT[:, 0, n * 512:(n + 1) * 512], ps[:, 6 + n, :], ACT.Copy).then_inc(xnT_copied, 1)
            for n in range(2):
                act.wait_ge(qT_ready, n + 1)
                run(qT[:, n * 512:(n + 1) * 512], ps[:, n, :], ACT.Identity, bias=cols[:, 0:1]).then_inc(qT_copied, 1)
            for t in range(NT):
                act.wait_ge(xs_max, t // 2 + 1)
                run(sc[:, t, :], sc[:, t, :], ACT.Exp, bias=smax[:, t:t + 1],
                    accum_out=ssum[:, t:t + 1]).then_inc(xs_exp, 1)
            for n in range(4):
                act.wait_ge(pT_ready, n + 1)
                run(pT[:, 2 * n:2 * n + 2, :, :].rearrange("p t j i -> p (t j i)"), ps[:, (6 + n) % 8, :],
                    ACT.Copy).then_inc(pT_copied, 1)
            for n in range(2):
                act.wait_ge(cT_ready, n + 1)
                run(cT[:, n * 512:(n + 1) * 512], ps[:, 2 + n, :], ACT.Copy).then_inc(cT_copied, 1)
            for n in range(2):
                act.wait_ge(xnT_ready, 3 + n)
                run(xnT[:, 1, n * 512:(n + 1) * 512], ps[:, 6 + n, :], ACT.Copy).then_inc(xnT_copied, 1)
            for n in range(2 * NO):
                act.wait_ge(gate_ready, n + 1)
                if n >= 2:
                    act.wait_ge(gate_done, n - 1)
                run(silu[:, n % 2, :], ps[:, n % 2 * 2, :], ACT.Silu,
                    scale=cols[:, 2 + n % NO:3 + n % NO]).then_inc(silu_done, 1)
            for bank0, dst, ready, done in ((4, 1, mid1_ready, mid1_done), (0, 2, mid2_ready, mid2_done)):
                for n in range(2 * NO):
                    th, o = n // NO, n % NO
                    act.wait_ge(ready, n + 1)
                    c0 = 2 + (1 + dst) * NO + o
                    run(hid[:, dst, o, th * 512:(th + 1) * 512], ps[:, bank0 + n % 4, :], ACT.Gelu,
                        scale=cols[:, c0:c0 + 1]).then_inc(done, 1)

        @block.gpsimd
        def _(pool):
            nc.gpsimd.memset(vw[:], 1.0).then_inc(ones_set, 1)
            nc.gpsimd.memset(half_pow[:], -0.5).then_inc(pool_step, 1)
            pool.wait_ge(pool_step, 1)
            for layer in range(3):
                for n in range(2):
                    pool.wait_ge(ln_var, 2 * layer + n + 1)
                    r = rstd[:, layer, 4 * n:4 * n + 4]
                    nc.gpsimd.tensor_scalar(r, mv[:, layer, 4 * n:4 * n + 4, 1], EPS, None, ALU.add
                                            ).then_inc(pool_step, 1)
                    pool.wait_ge(pool_step, 2 + 2 * layer + n)
                    nc.gpsimd.tensor_tensor(r, r, half_pow[:, 4 * n:4 * n + 4], ALU.pow).then_inc(ln_rstd, 1)

        @block.vector
        def _(dve):
            v = nc.vector
            steps = [0]

            def settle(ins):
                steps[0] += 1
                ins.then_inc(dve_step, 1)
                dve.wait_ge(dve_step, steps[0])

            def col(c):
                return con[:, c:c + 1]

            v.memset(q_st[:].rearrange("p a e b i -> p (a e b i)").bitcast(F32), 0.0).then_inc(zeros_set, 1)

            def cut_parts(whole, rest, parts):
                settle(v.tensor_copy(parts[0], whole))
                settle(v.tensor_tensor(rest, whole, parts[0], ALU.subtract))
                settle(v.tensor_copy(parts[1], rest))
                return v.tensor_tensor(parts[2], rest, parts[1], ALU.subtract)

            for half in range(2):
                for what in range(3):
                    dve.wait_ge(full_done, 3 * half + what + 1)
                    if what == 0:
                        whole, rest = full[:, half, 0, :], left[:, half, 0, :]
                        parts = [q_part[:, half, m, :] for m in range(3)]
                    else:
                        whole, rest = (t[:, half, what, :].rearrange("p (b j) -> p b j", b=2) for t in (full, left))
                        parts = [k_part[:, half, m, :, what - 1, :] for m in range(3)]
                    cut_parts(whole, rest, parts).then_inc(parts_done, 1)

            dve.wait_ge(ld_first, 16 * N_FIRST)
            settle(v.tensor_scalar(cut[:, 0, :], relraw[:], relraw[:, 0:1], None, ALU.subtract))
            settle(cut_parts(cut[:, 0, :], cut[:, 1, :], [cut_bf[:, 0, :], cut_bf[:, 1, :], cut[:, 2, :]]))
            settle(v.tensor_scalar(cut[:, 3, :], cut_bf[:, 0, :], col(HI), None, ALU.mult))
            settle(v.scalar_tensor_tensor(cut[:, 4, :], cut_bf[:, 1, :], col(MID), cut[:, 3, :], ALU.mult, ALU.add))
            v.scalar_tensor_tensor(table[:], cut[:, 2, :], col(LO), cut[:, 4, :],
                                   ALU.mult, ALU.add).then_inc(table_done, 1)

            dve.wait_ge(ones_set, 1)
            dve.wait_ge(ld_mid, 16 * N_MID)
            for b in range(B):
                dve.wait_ge(v_ready, 2 * b + 2)
                for half in range(2):
                    last = v.tensor_tensor(
                        vw_at[:, b, 1, half, :, :, 0:DK].rearrange("p h e d -> p e h d"),
                        ps[:, 5, half * S:(half + 1) * S].rearrange("p (e h d) -> p e h d", e=2, h=H),
                        rvfar[:, 2 * half:2 * half + 2, :].unsqueeze(2).to_broadcast([P, 2, H, DK]), ALU.add)
                last.then_inc(v_copied[1], 1)

            def maxima(b, half, g):
                u = (2 * b + half) * G + g
                for pair in range(2):
                    n, h = 2 * u + pair, K4 * g + 2 * pair
                    dve.wait_ge(nat_ready, n + 1)
                    v.tensor_reduce(mq[:, half, b, h:h + 2], ps[:, n % 2, :].rearrange("p (h j) -> p h j", h=2),
                                    AX.X, ALU.max).then_inc(nat_read, 1)
                dve.wait_ge(dist_ready, u + 1)
                v.tensor_reduce(mr[:, half, b, K4 * g:K4 * g + K4],
                                ps[:, 2, 0:K4 * 66].rearrange("p (h r) -> p h r", h=K4),
                                AX.X, ALU.max).then_inc(dist_read, 1)

            def shift(b):
                dve.wait_ge(dist_read, 8 * (b + 1))
                settle(v.scalar_tensor_tensor(negm[:, :, b, :], mq[:, :, b, :], -1.0, mr[:, :, b, :],
                                              ALU.mult, ALU.subtract))
                st = [negm_st[:, :, b, m * H:(m + 1) * H].rearrange("p f (e a) -> p f a e", e=2) for m in range(3)]

                def by_pair(t):
                    return t.rearrange("p f (a e) -> p f a e", e=2)

                whole, rest = negm[:, :, b, :], negm_left[:, :, b, :]
                bf = [negm_bf[:, m, :, b, :] for m in range(2)]
                settle(cut_parts(whole, rest, [bf[0], bf[1], negm[:, :, b, :]]))
                v.tensor_copy(st[0], by_pair(bf[0]))
                v.tensor_copy(st[1], by_pair(bf[1]))
                settle(v.tensor_copy(st[2], by_pair(negm[:, :, b, :])))
                dve.nop().then_inc(negm_done, 1)

            def add_relative(q, b, half, g):
                dve.wait_ge(near_ready, q + 1)
                if q == 0:
                    dve.wait_ge(rel_copied, S // 8)
                tile = heads_of(near, b, half, g)
                v.tensor_tensor(tile, ps[:, 3 + q % 2, :].rearrange("p (k i) -> p k i", k=K4), tile,
                                ALU.add).then_inc(near_added, 1)

            def copy_values(q, b, half):
                dve.wait_ge(pv_done, q + 1)
                for e in range(2):
                    r = slice(e * BLK, (e + 1) * BLK)
                    last = v.tensor_copy(pvs[r, half, b * H:(b + 1) * H, :],
                                         ps[r, 7, 0:2 * VC * H].rearrange("p (h e d) -> p h e d", e=2, d=VC)[:, :, e, :])
                last.then_inc(pv_copied, 1)

            for b in range(2):
                for half in range(2):
                    for g in range(G):
                        maxima(b, half, g)
                shift(b)
            for q, b, half, g in units():
                add_relative(q, b, half, g)
                if b + 2 < B:
                    maxima(b + 2, half, g)
                if q % G == 1 and q > G:
                    copy_values(q - 2, (q - 2) // 8, (q - 2) // G % 2)
                if q % 8 == 7 and b + 2 < B:
                    shift(b + 2)
            copy_values(4 * 8 - 1, B - 1, 1)

            for n in range(8):
                dve.wait_ge(relv_ready, n + 1)
                v.tensor_copy(rvo[:, 32 * n:32 * (n + 1):2, :],
                              ps[0:BH, n % 4, 0:32 * DK].rearrange("p (i e d) -> p i e d", e=2, d=DK)[:, :, 1, :]
                              ).then_inc(relv_even, 1)

            dve.wait_ge(pv_copied, 2 * B)
            settle(v.reciprocal(lsum[:], pvs[:, :, :, DK]))
            for half in range(2):
                dve.wait_ge(relv_turned, half + 1)
                for b in range(B):
                    turned = ps[:, 4 + half, :].rearrange("p (d h b) -> p b h d", d=DK, b=B)[:, b]
                    last = v.tensor_tensor(num[:, half, b * H:(b + 1) * H, :], turned,
                                           pvs[:, half, b * H:(b + 1) * H, 0:DK], ALU.add)
                settle(last)
                v.tensor_tensor(catt[:, half], num[:, half], lsum[:, half, :].unsqueeze(2).to_broadcast([P, BH, DK]),
                                ALU.mult).then_inc(catt_done, 1)

            dve.wait_ge(ld_late, 16 * N_LATE)
            dve.wait_ge(ld_weights, 16 * N_WEIGHTS)
            v.tensor_scalar(keep[:], mask_sb[:], 0.0, None, ALU.not_equal)
            v.tensor_scalar(pen[:], mask_sb[:], 0.0, NEG, ALU.is_equal, ALU.mult)
            for n in range(2):
                dve.wait_ge(xv_ready, n + 1)
                v.tensor_tensor(v_nat[:, 4 * n:4 * n + 4, :], ps[:, 2 + n, :].rearrange("p (t d) -> p t d", t=4),
                                rows[:, 1:2, :].to_broadcast([P, 4, D]), ALU.add).then_inc(xv_copied, 1)

            def residual(base, bias_row):
                settle(v.tensor_tensor(xb[:], base, rows[:, bias_row:bias_row + 1, :].to_broadcast([P, NT, D]),
                                       ALU.add))

            def norm(layer, ready, count, scale=None):
                for n in range(2):
                    dve.wait_ge(ready, count + n + 1)
                    t0 = slice(4 * n, 4 * n + 4)
                    src = ps[:, 4 + n, :].rearrange("p (t d) -> p t d", t=4)
                    if scale is not None:
                        settle(v.tensor_tensor(y[:, t0, :], src, scale, ALU.mult))
                        src = y[:, t0, :]
                    settle(v.tensor_tensor(y[:, t0, :], src, (xb if layer < 2 else xn[:, 1])[:, t0, :], ALU.add))
                    for t in range(4 * n, 4 * n + 4):
                        last = v.bn_stats(stats[:, t, :], y[:, t, :])
                    settle(last)
                    for t in range(4 * n, 4 * n + 4):
                        last = v.bn_aggr(mv[:, layer, t, :], stats[:, t, :])
                    last.then_inc(ln_var, 1)
                    dve.wait_ge(ln_rstd, 2 * layer + n + 1)
                    for t in range(4 * n, 4 * n + 4):
                        v.tensor_scalar(xn[:, layer, t, :], y[:, t, :], mv[:, layer, t, 0:1],
                                        rstd[:, layer, t:t + 1], ALU.subtract, ALU.mult).then_inc(xn_done, 1)

            residual(x_nat[:], 0)
            norm(0, att_ready, 0)
            dve.wait_ge(xn_done, NT)
            residual(xn[:, 0], 2)
            for n in range(4):
                dve.wait_ge(xs_ready, n + 1)
                two = slice(2 * n, 2 * n + 2)
                settle(v.scalar_tensor_tensor(sc[:, two, :], ps[:, 2 + n, :].rearrange("p (t j) -> p t j", t=2),
                                              float(D) ** -0.5, keep[:, two, :], ALU.mult, ALU.mult))
                settle(v.tensor_tensor(sc[:, two, :], sc[:, two, :], pen[:, two, :], ALU.add))
                v.tensor_reduce(smax[:, two], sc[:, two, :], AX.X, ALU.max, negate=True).then_inc(xs_max, 1)
            for t in range(NT):
                dve.wait_ge(xs_exp, t + 1)
                settle(v.reciprocal(srec[:, t:t + 1], ssum[:, t:t + 1]))
                v.tensor_scalar(sc[:, t, :], sc[:, t, :], srec[:, t:t + 1], None, ALU.mult).then_inc(xs_norm, 1)
            norm(1, att_ready, 2)

            for n in range(2 * NO):
                th, o = n // NO, n % NO
                dve.wait_ge(silu_done, n + 1)
                v.scalar_tensor_tensor(hid[:, 0, o, th * 512:(th + 1) * 512], ps[:, n % 2 * 2 + 1, :],
                                       cols[:, 2 + NO + o:3 + NO + o], silu[:, n % 2, :],
                                       ALU.mult, ALU.mult).then_inc(gate_done, 1)
            norm(2, ffn_ready, 0, rows[:, 3:4, :].to_broadcast([P, 4, D]))


def kernel(**inputs):
    import ml_dtypes
    import numpy as np
    import concourse.bacc as bacc
    from concourse.bass_utils import run_bass_kernel_spmd

    a = {k.replace("L0_", ""): np.asarray(v) for k, v in inputs.items()}
    tokens = a["x"].reshape(TOK, D)
    around = [j % S for j in range(HALO)]
    clipped = [min(max(u - (P - 1), -MAX_REL), MAX_REL) + MAX_REL for u in range(2 * P + WIDE // DK)]
    far_rows = [[(0 if (w + P) + c >= S else NREL - 1) for w in WIN] for c in range(P)]
    consts = np.zeros((P, P + 8), np.float32)
    consts[:, :P] = np.eye(P, dtype=np.float32)
    for r in range(P):
        if r % BLK < SHIFT:
            consts[r, HI + STACK[r % BLK // DK][1]] = 1

    def columns(s):
        return s.reshape(-1, P).T

    arrays = dict(
        x=tokens, xT=a["x"].transpose(2, 0, 1)[:, :, around],
        ctxT=a["ctx_1024"].reshape(TOK, D).T, mask=a["mask_BxSxS2_if1"].reshape(TOK, S),
        consts=consts, ones=np.ones(PAIRS * B * 2 * S, ml_dtypes.bfloat16),
        wqT=a["attn_Wq"].T, wkT=a["attn_Wk"].T, wvT=a["attn_Wv"].T, woT=a["attn_Wo"].T, b_o=a["attn_b_o"],
        relk=np.tile(a["attn_rel_k_emb"][clipped[:2 * P]].T, (H, 1)),
        relv=a["attn_rel_v_emb"][clipped], relv_far=a["attn_rel_v_emb"][far_rows],
        xwq=a["xattn_Wq"].T, xbq=a["xattn_bq"].reshape(D, 1), xwk=a["xattn_Wk"].T, xbk=a["xattn_bk"].reshape(D, 1),
        xwv=a["xattn_Wv"].T, xbv=a["xattn_bv"], xwo=a["xattn_Wo"].T, xbo=a["xattn_bo"],
        w1=a["ffn_w1_w"].T, s1=columns(a["ffn_w1_s"]), w2=a["ffn_w2_w"].T, s2=columns(a["ffn_w2_s"]),
        h1=a["ffn_h1_w"].T, hs=np.concatenate([columns(a["ffn_h1_s"]), columns(a["ffn_h2_s"])], 1),
        h2=a["ffn_h2_w"].T, w3=a["ffn_w3_w"].T, s3=a["ffn_w3_s"])
    arrays = {k: np.ascontiguousarray(v) for k, v in arrays.items()}

    nc = bacc.Bacc("TRN2", target_bir_lowering=False, num_devices=1)
    ap = {k: nc.dram_tensor("in_" + k, v.shape, mybir.dt.from_np(v.dtype), kind="ExternalInput").ap()
          for k, v in arrays.items()}
    result = nc.dram_tensor("out", (TOK, D), F32, kind="ExternalOutput").ap()
    build(nc, *(ap.get(n) for n in (
        "x", "xT", "ctxT", "mask", "consts", "ones", "wqT", "wkT", "wvT", "woT", "b_o", "relk", "relv", "relv_far",
        "xwq", "xbq", "xwk", "xbk", "xwv", "xbv", "xwo", "xbo",
        "w1", "s1", "w2", "s2", "h1", "hs", "h2", "w3", "s3")), result)
    r = run_bass_kernel_spmd(nc, [{"in_" + k: v for k, v in arrays.items()}], core_ids=[0])
    return r.results[0]["out"].reshape(B, S, D)
```

```python
from contextlib import ExitStack

import concourse.bass as bass
from concourse import mybir

F32 = mybir.dt.float32
BF16 = mybir.dt.bfloat16
F32R = mybir.dt.float32r
I32 = mybir.dt.int32
ALU = mybir.AluOpType
ACT = mybir.ActivationFunctionType
AX = mybir.AxisListType

P = 128
B, S, D = 4, 256, 128
H, DK = 16, 8
G, K4 = 4, 4
PAIRS = H // 2
STACK = [(0, 0), (0, 1), (0, 2), (1, 0), (1, 1), (2, 0)]
SHIFT = len(STACK) * DK
WIDE = 128
TOK = B * S
NT = TOK // P
HID = 512
NO = HID // P
MAX_REL = 32
NREL = 2 * MAX_REL + 1
BLK = 64
WIN = [0, 32, 96, 128]
VWIN = WIN + [(w + P) % S for w in WIN]
EPS = 1e-5
NEG = -1.0e30
PASSES = [(0, 0), (0, 1), (1, 0)]
BF16_ONES = 1 + 0x3F80 / 2 ** 23
HALO = 384
BH = B * H
VC = DK + 1

HI, MID, LO = range(P, P + 3)
LAST, FIRST = P + 3, P + 4

WQ, WK, WV, WO = range(4)
ROW_BO, ROW_XBV, ROW_XBO, ROW_S3 = range(4)
COL_XBQ, COL_XBK, COL_S1, COL_S2, COL_H1, COL_H2 = 0, 1, 2, 2 + NO, 2 + 2 * NO, 2 + 3 * NO


def build(nc, x, xT, ctxT, mask, consts, w_self, relk, relv, relv_far, w_cross, vectors, columns,
          w1, w2, h1, h2, w3, out):
    with ExitStack() as ctx:
        def sb(name, shape, dt=F32, stack=ctx):
            return stack.enter_context(nc.sbuf_tensor(name, shape, dt))

        def sem(name):
            return ctx.enter_context(nc.semaphore(name))

        ps = ctx.enter_context(nc.psum_tensor("ps", [P, 8, 512], F32))

        con = sb("con", [P, P + 8])
        ident = con[:, 0:P]
        w_sb = sb("w_sb", [P, 4, D])
        xw_sb = sb("xw_sb", [P, 4, D])
        rows = sb("rows", [P, 4, D])
        cols = sb("cols", [P, 2 + 4 * NO])
        kT = sb("kT", [P, TOK])
        v_nat = sb("v_nat", [P, NT, D])
        rv = sb("rv", [P, P * DK + WIDE - 2 * DK])
        pvs = sb("pvs", [P, 2, BH, VC])
        silu = sb("silu", [P, 2, 512])
        lsum = sb("lsum", [P, 2, BH])
        smax = sb("smax", [P, NT])
        ssum = sb("ssum", [P, NT])
        srec = sb("srec", [P, NT])
        half_pow = sb("half_pow", [P, NT])
        mv = sb("mv", [P, 3, NT, 2])
        rstd = sb("rstd", [P, 3, NT])
        stats = sb("stats", [P, NT, 6])

        with ExitStack() as first_batches:
            k_st = [sb("k_st0", [P, PAIRS, 2, 2 * S], BF16, stack=first_batches)]
        xb = sb("xb", [P, 2, NT, D])
        y = sb("y", [P, NT, D])
        xn0 = sb("xn0", [P, NT, D])

        with ExitStack() as projecting:
            relraw = sb("relraw", [P, 2 * P], stack=projecting)
            cut_bf = sb("cut_bf", [P, 2, 2 * P], BF16, stack=projecting)
            q_part = sb("q_part", [P, 2, 3, 512], BF16, stack=projecting)
            k_part = sb("k_part", [P, 2, 2, 3, 512], BF16, stack=projecting)
        far = sb("far", [P, 2, 512])
        catt = sb("catt", [P, 2, BH, DK])
        cattT = sb("cattT", [P, TOK])
        sc = sb("sc", [P, NT, S])

        early = ExitStack()
        table = sb("table", [P, 2 * P], BF16, stack=early)
        rvfar = sb("rvfar", [P, 4, DK], stack=early)
        q_st = sb("q_st", [P, PAIRS, 2, B, S], BF16, stack=early)
        k_st.append(sb("k_st1", [P, PAIRS, 2, 2 * S], BF16, stack=early))
        V_RUN = 2 * B * 2 * H * 2 * VC
        vw = sb("vw", [P, V_RUN + WIDE - 2 * VC], stack=early)
        vw_at = vw[:, 0:V_RUN].rearrange("p (b s f h e d) -> p b s f h e d", b=B, s=2, f=2, h=H, e=2)
        mq = sb("mq", [P, 2, B, H], stack=early)
        mr = sb("mr", [P, 2, B, H], stack=early)
        negm = sb("negm", [P, 2, B, H], stack=early)
        negm_left = sb("negm_left", [P, 2, B, H], stack=early)
        negm_bf = sb("negm_bf", [P, 2, 2, B, H], BF16, stack=early)
        negm_st = sb("negm_st", [P, 2, B, 3 * H], stack=early)
        mt = sb("mt", [3 * H, B, S], BF16, stack=early)
        with ExitStack() as big:
            near = sb("near", [P, S, BH], stack=big)
        with ExitStack() as big:
            hid = sb("hid", [P, 2, 2, 2, NO, 512], F32R, stack=big)
        early.close()

        mask1_sb = sb("mask1_sb", [P, B, S], I32)
        W_ALL = 2 * HID + 2 * NO * HID
        with ExitStack() as whole:
            w_whole = sb("w_whole", [P, W_ALL], stack=whole)
        w_part = [sb("w_lower", [P, W_ALL], F32R)]
        w_part.insert(0, sb("w_upper", [P, W_ALL], F32R))
        W1, W2, H1, H2 = 0, HID, 2 * HID, 2 * HID + NO * HID
        w3_sb = sb("w3_sb", [P, NO, D])
        xn12 = sb("xn12", [P, 2, NT, D])
        xn = [xn0[:], xn12[:, 0], xn12[:, 1]]
        x2T = sb("x2T", [P, 2, TOK], F32R)
        xnT = [catt[:].rearrange("p f m d -> p (f m d)"), cattT]
        qT = cattT
        mask_in = [silu[:].rearrange("p n (t j) -> p (n t) j", j=S).bitcast(I32), mask1_sb[:]]
        pen = [silu[:].rearrange("p n (t j) -> p (n t) j", j=S), mask1_sb[:].bitcast(F32)]
        rvo = sc[0:BH].rearrange("p t j -> p (t j)").rearrange("p (i d) -> p i d", d=DK)
        gelu_out = sc[:].rearrange("p t j -> p (t j)").rearrange("p (o t) -> p o t", o=NO)
        flat = near[:, :, :].rearrange("p i m -> p (i m)")
        left = flat[:, 0:2 * 512].rearrange("p (n t) -> p n t", n=2)
        at = 2 * 512
        cut = flat[:, at:at + 5 * 2 * P].rearrange("p (n u) -> p n u", n=5)
        at += 5 * 2 * P
        xT_sb = flat[:, at:at + B * HALO].rearrange("p (b j) -> p b j", b=B)
        ctx_sb = flat[:, at + B * HALO:at + B * HALO + TOK]
        at = NO * TOK
        hid3 = flat[:, 0:NO * TOK].rearrange("p (f o t) -> p f o t", f=2, o=NO)
        pT = flat[:, at:at + 2 * TOK].rearrange("p (t j i) -> p t j i", t=NT, j=2)
        cT = flat[:, at + 2 * TOK:at + 3 * TOK]

        q_way = nc.dram_tensor("q_way", [2, len(STACK), D, 512], BF16, kind="Internal").ap()
        k_way = nc.dram_tensor("k_way", [2, 2, 3, D, 512], BF16, kind="Internal").ap()
        m_way = nc.dram_tensor("m_way", [B, 3, 2, PAIRS, S], BF16, kind="Internal").ap()

        ld_x = [sem(f"ld_x{n}") for n in range(2)]
        ld_table, ld_cross, ld_relv = sem("ld_table"), sem("ld_cross"), sem("ld_relv")
        ld_x_nat, ld_rv = sem("ld_x_nat"), sem("ld_rv")
        ld_mask = [sem(f"ld_mask{f}") for f in range(2)]
        ld_gates, ld_h1, ld_h2, ld_w3 = sem("ld_gates"), sem("ld_h1"), sem("ld_h2"), sem("ld_w3")
        mask_turned, xb_done, w3_scaled = sem("mask_turned"), sem("xb_done"), sem("w3_scaled")
        proj_ready, upper_done, parts_done = sem("proj_ready"), sem("upper_done"), sem("parts_done")
        k_ones_set, zeros_set = sem("k_ones_set"), sem("zeros_set")
        parts_out = [sem(f"parts_out{n}") for n in range(6)]
        stacked = [sem(f"stacked{n}") for n in range(6)]
        zeros_set_pool, far_valued, xv_biased = sem("zeros_set_pool"), sem("far_valued"), sem("xv_biased")
        dve_step = sem("dve_step")
        ones_set, v_ready = sem("ones_set"), sem("v_ready")
        v_copied = [sem("v_copied_win"), sem("v_copied_far")]
        table_done = sem("table_done")
        rel_ready, rel_copied = sem("rel_ready"), sem("rel_copied")
        nat_ready, nat_read = sem("nat_ready"), sem("nat_read")
        dist_ready, dist_read = sem("dist_ready"), sem("dist_read")
        negm_done, negm_turned, negm_copied = sem("negm_done"), sem("negm_turned"), sem("negm_copied")
        shift_out = [sem(f"shift_out{b}") for b in range(B)]
        shift_placed = [sem(f"shift_placed{b}") for b in range(B)]
        near_ready, far_ready, near_added = sem("near_ready"), sem("far_ready"), sem("near_added")
        exp_near, exp_far = sem("exp_near"), sem("exp_far")
        pv_done, pv_copied = sem("pv_done"), sem("pv_copied")
        relv_ready, relv_even, relv_odd = sem("relv_ready"), sem("relv_even"), sem("relv_odd")
        relv_turned, catt_done = sem("relv_turned"), sem("catt_done")
        cattT_ready, cattT_copied = sem("cattT_ready"), sem("cattT_copied")
        kT_ready, kT_copied = sem("kT_ready"), sem("kT_copied")
        xv_ready, xv_copied = sem("xv_ready"), sem("xv_copied")
        att_ready, xatt_ready = sem("att_ready"), sem("xatt_ready")
        ln_var, ln_rstd, pool_step = sem("ln_var"), sem("ln_rstd"), sem("pool_step")
        xn_done, xnT_ready, xnT_copied = sem("xn_done"), sem("xnT_ready"), sem("xnT_copied")
        qT_ready, qT_copied = sem("qT_ready"), sem("qT_copied")
        xs_ready, xs_max, xs_exp = sem("xs_ready"), sem("xs_max"), sem("xs_exp")
        pT_ready, pT_copied = sem("pT_ready"), sem("pT_copied")
        cT_ready, cT_copied = sem("cT_ready"), sem("cT_copied")
        gate_ready, silu_done, gate_done = sem("gate_ready"), sem("silu_done"), sem("gate_done")
        gate_read, x2_cut, mid1_cut, weights_cut = sem("gate_read"), sem("x2_cut"), sem("mid1_cut"), sem("weights_cut")
        mid1_ready, mid1_done = sem("mid1_ready"), sem("mid1_done")
        mid2_ready, mid2_done = sem("mid2_ready"), sem("mid2_done")
        ffn_ready, stored = sem("ffn_ready"), sem("stored")

        N_TABLE, N_CROSS = 2, 4
        N_Q_WAYS, N_Q_STACK = 3, 2
        N_K_WAYS, N_K_STACK = 1, 6
        CUTS = [("q", 0, 0), ("k", 1, 0), ("q", 0, 1), ("k", 1, 1), ("k", 0, 0), ("k", 0, 1)]
        Q_CUT = [CUTS.index(("q", 0, half)) for half in range(2)]
        K_CUT = [[CUTS.index(("k", side, half)) for half in range(2)] for side in range(2)]

        def heads_of(near, b, half, g):
            return near[:, half * P:(half + 1) * P, :].rearrange("p i (h b) -> p b h i", b=B)[
                :, b, K4 * g:K4 * g + K4, :]

        def units():
            for q in range(B * 2 * G):
                yield q, q // 8, q // G % 2, q % G

        Q_ZERO = 6
        REL_AFTER = [0, 3, 3, 3, 3, 3, 3, 6, 4, 4, 0, 0]
        AHEAD = len(REL_AFTER)

        def natural_unit(n):
            return n // (2 * G), n // G % 2, n % G

        def maxima_at(q):
            return (q + AHEAD) // 8 - 1 if (q + AHEAD) % 8 == 0 and q + AHEAD <= 4 * 8 else None

        assert sum(REL_AFTER) == S // 8

        BANKS = ((0, 1, 2, 3), (4, 5, 6, 7))
        REL_BANK = (0, 1, 2, 0, 4, 5, 6, 7)
        NORMS = [(0, 0), (1, 0), (0, 1), (1, 1), (2, 0), (2, 1)]
        FIRST_UNITS = 4 * 8 - 4
        LAST_UNITS = [u for u in units() if u[0] >= FIRST_UNITS]

        block = ctx.enter_context(nc.Block())

        @block.sync
        def _(sp):
            sp.dma_start(w_sb[:], w_self).then_inc(ld_x[0], 16)
            for n in range(2):
                sp.dma_start(xT_sb[:, 2 * n:2 * n + 2, :], xT[:, 2 * n:2 * n + 2, :]).then_inc(ld_x[n], 16)
            for dst, src in ((con, consts), (relraw, relk)):
                sp.dma_start(dst[:], src).then_inc(ld_table, 16)
            for dst, src in ((ctx_sb, ctxT), (xw_sb[:], w_cross), (cols[:], columns),
                             (rows[:], vectors.partition_broadcast(P))):
                sp.dma_start(dst, src).then_inc(ld_cross, 16)
            sp.dma_start(rvfar[:], relv_far).then_inc(ld_relv, 16)

            def write_parts(c):
                what, side, half = CUTS[c]
                sp.wait_ge(parts_done, c + 1)
                if what == "k":
                    sp.dma_start(k_way[side, half].rearrange("m c t -> c m t"),
                                 k_part[:, side, half]).then_inc(parts_out[c], 16)
                    return
                for part in range(3):
                    p0, n = [p for p, _ in STACK].index(part), 3 - part
                    sp.dma_start(q_way[half, p0:p0 + n].rearrange("p c t -> c p t"),
                                 q_part[:, half, part:part + 1, :].to_broadcast([P, n, 512])
                                 ).then_inc(parts_out[c], 16)

            def stack_parts(c):
                what, side, half = CUTS[c]
                sp.wait_ge(parts_out[c], 16 * (N_K_WAYS if what == "k" else N_Q_WAYS))
                if c == 0:
                    sp.wait_ge(zeros_set, 1)
                    sp.wait_ge(zeros_set_pool, 1)
                if what == "k" and side == 1:
                    sp.wait_ge(k_ones_set, half + 1)
                for e in range(2):
                    if what == "q":
                        r = slice(e * BLK, e * BLK + SHIFT)
                        sp.dma_start(q_st[r, :, e, 2 * half:2 * half + 2, :].rearrange("r a b i -> r a (b i)"),
                                     q_way[half].rearrange("p (d e a) t -> e (p d) a t", e=2, a=PAIRS)[e]
                                     ).then_inc(stacked[c], 16)
                        continue
                    for run in range(3):
                        p0, n = [p for p, _ in STACK].index(run), 3 - run
                        r = slice(e * BLK + p0 * DK, e * BLK + (p0 + n) * DK)
                        sp.dma_start(k_st[half][r, :, :, side * S:(side + 1) * S].rearrange("r a b i -> r (a b) i"),
                                     k_way[side, half, 0:n].rearrange(
                                         "p (d e a) (b i) -> e (p d) (a b) i", e=2, a=PAIRS, b=2)[e]
                                     ).then_inc(stacked[c], 16)

            for c in range(3):
                write_parts(c)
            for c in range(3):
                stack_parts(c)
            write_parts(3)
            stack_parts(3)
            write_parts(4)
            write_parts(5)
            stack_parts(4)
            stack_parts(5)
            slide = bass.AP(relv.tensor, 0, [[DK, P], [1, P * DK + WIDE - 2 * DK]])
            sp.dma_start(rv[:], slide).then_inc(ld_rv, 16)

            for b in range(B):
                sp.wait_ge(negm_copied, b + 1)
                sp.dma_start(m_way[b].rearrange("m e a i -> (m e a) i"), mt[:, b, :]).then_inc(shift_out[b], 16)
                sp.wait_ge(shift_out[b], 16)
                if b == 0:
                    sp.wait_ge(rel_ready, S // 8)
                for e in range(2):
                    r = e * BLK + SHIFT
                    sp.dma_start(q_st[r:r + 3, :, e, b, :], m_way[b, :, e]).then_inc(shift_placed[b], 16)

            sp.wait_ge(pv_done, 2 * 8)
            for f in range(2):
                sp.dma_start(xb[:, 0, 4 * f:4 * f + 4, :],
                             x.rearrange("(b f p) d -> f p b d", f=2, p=P)[f]).then_inc(ld_x_nat, 16)
            masks = mask.rearrange("(b f p) j -> f p b j", f=2, p=P)
            sp.dma_start(mask_in[0], masks[0]).then_inc(ld_mask[0], 16)
            sp.wait_ge(pv_done, 4 * 8)
            sp.dma_start(w_whole[:, W1:W2], w1).then_inc(ld_gates, 16)
            sp.dma_start(w_whole[:, W2:H1], w2).then_inc(ld_gates, 16)
            for c, h, done in ((H1, h1, ld_h1), (H2, h2, ld_h2)):
                sp.dma_start(w_whole[:, c:c + NO * HID].rearrange("p (k o) -> p k o", k=NO),
                             h.rearrange("(k p) o -> p k o", p=P)).then_inc(done, 16)
            sp.dma_start(mask_in[1], masks[1]).then_inc(ld_mask[1], 16)
            sp.dma_start(w3_sb[:], w3.rearrange("(k p) o -> p k o", p=P)).then_inc(ld_w3, 16)

            for f, b0, n in ((0, 0, 4), (1, 0, 2), (1, 2, 2)):
                t = 4 * f + b0
                sp.wait_ge(xn_done, 4 * NORMS.index((2, f)) + b0 + n)
                sp.dma_start(out.rearrange("(b f p) d -> f p b d", f=2, p=P)[f, :, b0:b0 + n, :],
                             xn[2][:, t:t + n, :]).then_inc(stored, 16)
            sp.wait_ge(stored, 16 * 3)

        @block.tensor
        def _(pe):
            mm, turn = nc.tensor.matmul, nc.tensor.transpose

            for n in range(4):
                if n % 2 == 0:
                    pe.wait_ge(ld_x[n // 2], 16 * (2 - n // 2))
                mm(ps[:, n, :], w_sb[:, (WQ, WK)[n % 2], :], xT_sb[:, n // 2 * 2:n // 2 * 2 + 2, 0:S],
                   start=True, stop=True).then_inc(proj_ready, 1)

            pe.wait_ge(ld_cross, 16 * N_CROSS)
            for n in range(2):
                mm(ps[:, 6 + n, :], xw_sb[:, WK, :], ctx_sb[:, n * 512:(n + 1) * 512],
                   start=True, stop=True).then_inc(kT_ready, 1)

            for n in range(2 * B):
                b, side = n // 2, n % 2
                if n >= 2:
                    pe.wait_ge(v_copied[side], n // 2)
                for w in range(4):
                    j0 = VWIN[4 * side + w]
                    last = mm(ps[:, 4 + n % 2, w * D:(w + 1) * D], xT_sb[:, b, j0:j0 + P], w_sb[:, WV, :],
                              start=True, stop=True)
                last.then_inc(v_ready, 1)

            for n in range(2):
                pe.wait_ge(v_copied[n], B)
                for e in range(4):
                    t = 4 * n + e
                    last = mm(ps[:, 4 + n, e * D:(e + 1) * D], ctx_sb[:, t * P:(t + 1) * P], xw_sb[:, WV, :],
                              start=True, stop=True)
                last.then_inc(xv_ready, 1)

            def relative(n):
                if n == 0:
                    pe.wait_ge(stacked[Q_CUT[1]], 16 * N_Q_STACK)
                    pe.wait_ge(kT_copied, 2)
                    pe.wait_ge(xv_copied, 2)
                if n >= 4:
                    pe.wait_ge(rel_copied, n - 3)
                for e in range(8):
                    i = 8 * n + e
                    o = i - WIN[i // BLK]
                    last = mm(ps[:, 4 + n % 4, e * BH:(e + 1) * BH], table[:, P - 1 - o:2 * P - 1 - o],
                              q_st[:, :, :, :, i].rearrange("p a e b -> p (a e b)"), start=True, stop=True)
                last.then_inc(rel_ready, 1)

            def natural(b, half, g):
                u = (2 * b + half) * G + g
                if u == 8:
                    pe.wait_ge(stacked[K_CUT[1][1]], 16 * N_K_STACK)
                for pair in range(2):
                    n = 2 * u + pair
                    if n >= 2:
                        pe.wait_ge(nat_read, n - 1)
                    for e in range(2):
                        last = mm(ps[:, n % 2, e * S:(e + 1) * S],
                                  q_st[:, 2 * g + pair, e, b, half * P:(half + 1) * P],
                                  k_st[b // 2][:, 2 * g + pair, b % 2, S:2 * S], start=True, stop=True)
                    last.then_inc(nat_ready, 1)
                if u >= 1:
                    pe.wait_ge(dist_read, u)
                if half == 0 and g == 0 and b >= 1:
                    pe.wait_ge(negm_copied, b)
                for k in range(K4):
                    last = mm(ps[:, 2, k * 66:k * 66 + 66],
                              q_st[:, 2 * g + k // 2, k % 2, b, half * P:(half + 1) * P],
                              table[:, P - 1 - MAX_REL:P - 1 - MAX_REL + 66], start=True, stop=True)
                last.then_inc(dist_ready, 1)

            def turn_maxima(b):
                pe.wait_ge(negm_done, b + 1)
                for half in range(2):
                    last = turn(ps[0:3 * H, 2, half * P:(half + 1) * P], negm_st[:, half, b, :], ident)
                last.then_inc(negm_turned, 1)

            def scores(q, b, half, g):
                if q == 0:
                    pe.wait_ge(rel_copied, S // 8)
                if q % 8 == 0:
                    pe.wait_ge(shift_placed[b], 16 * 2)
                    pe.wait_ge(stacked[K_CUT[0][b // 2]], 16 * N_K_STACK)
                if q >= 2:
                    pe.wait_ge(near_added, q - 1)
                    pe.wait_ge(exp_far, q - 1)
                for what, bank, done in ((0, 3 + q % 2, near_ready), (1, 5 + q % 2, far_ready)):
                    for pair in range(2):
                        for e in range(2):
                            blk = 2 * half + e
                            j0 = (S + WIN[blk], WIN[blk] + P)[what]
                            o = ps[:, bank, pair * S:(pair + 1) * S].rearrange(
                                "p (k f i) -> p k f i", k=2, f=2)[:, :, e, :]
                            last = mm(o, k_st[b // 2][:, 2 * g + pair, b % 2, j0:j0 + P],
                                      q_st[:, 2 * g + pair, :, b, blk * BLK:(blk + 1) * BLK],
                                      start=True, stop=True)
                    last.then_inc(done, 1)

            def vw_run(b, side, half, h):
                at = (((b * 2 + side) * 2 + half) * H + h) * 2 * VC
                return vw[:, at:at + WIDE]

            def values(q, b, half, g):
                pe.wait_ge(exp_near, q + 1)
                pe.wait_ge(exp_far, q + 1)
                if g == 0:
                    if q == 0:
                        pe.wait_ge(far_valued, B)
                    else:
                        pe.wait_ge(pv_copied, q // G)
                for k in range(K4):
                    h = K4 * g + k
                    o = ps[:, 7, h * 2 * VC:h * 2 * VC + WIDE]
                    mm(o, near[:, half * P:(half + 1) * P, h * B + b], vw_run(b, 0, half, h),
                       start=True, stop=False)
                    last = mm(o, far[:, q % 2, k * P:(k + 1) * P], vw_run(b, 1, half, h),
                              start=False, stop=True)
                last.then_inc(pv_done, 1)

            pe.wait_ge(parts_done, len(CUTS))
            pe.wait_ge(stacked[Q_CUT[0]], 16 * N_Q_STACK)
            pe.wait_ge(stacked[K_CUT[1][0]], 16 * N_K_STACK)
            pe.wait_ge(table_done, 1)
            n = 0
            for u in range(AHEAD):
                natural(*natural_unit(u))
                for _ in range(REL_AFTER[u]):
                    relative(n)
                    n += 1
                if u == 2 * G - 1:
                    turn_maxima(0)
            before = None
            for q, b, half, g in list(units())[:FIRST_UNITS]:
                scores(q, b, half, g)
                complete = maxima_at(q)
                if complete is None and q + AHEAD < 4 * 8:
                    natural(*natural_unit(q + AHEAD))
                if before:
                    values(*before)
                if complete is not None:
                    turn_maxima(complete)
                    if q + AHEAD < 4 * 8:
                        natural(*natural_unit(q + AHEAD))
                before = (q, b, half, g)
            values(*before)

            def relative_values(job):
                if job == 3:
                    pe.wait_ge(relv_even, 1)
                    pe.wait_ge(relv_odd, 1)
                if job == 7:
                    pe.wait_ge(pv_copied, 2 * B)
                for e in range(16):
                    n = 16 * job + e
                    o = 2 * n - WIN[2 * n // BLK]
                    r0 = (P - 2 - o) * DK
                    last = mm(ps[:, REL_BANK[job], e * 2 * DK:e * 2 * DK + WIDE],
                              near[:, 2 * n:2 * n + 2, :].rearrange("p i m -> p (i m)"),
                              rv[:, r0:r0 + WIDE], start=True, stop=True)
                last.then_inc(relv_ready, 1)

            def turn_relative_values(f):
                pe.wait_ge(relv_even, 4 * f + 4)
                pe.wait_ge(relv_odd, 4 * f + 4)
                for d in range(DK):
                    last = turn(ps[:, BANKS[f][0], d * BH:(d + 1) * BH], rvo[:, f * P:(f + 1) * P, d],
                                con[0:BH, 0:BH])
                last.then_inc(relv_turned, 1)

            def turn_heads(f):
                pe.wait_ge(catt_done, f + 1)
                for b in range(B):
                    last = turn(ps[:, BANKS[f][1], b * P:(b + 1) * P],
                                catt[:, f, b * H:(b + 1) * H, :].rearrange("p h d -> p (h d)"), ident)
                last.then_inc(cattT_ready, 1)

            def attention_out(f):
                pe.wait_ge(cattT_copied, f + 1)
                for b in range(B):
                    t = 4 * f + b
                    last = mm(ps[:, BANKS[f][0], b * D:(b + 1) * D], cattT[:, t * P:(t + 1) * P], w_sb[:, WO, :],
                              start=True, stop=True)
                last.then_inc(att_ready, 1)

            def turn_x(layer, f):
                for b in range(B):
                    t = 4 * f + b
                    pe.wait_ge(xn_done, 4 * NORMS.index((layer, f)) + b + 1)
                    last = turn(ps[:, BANKS[f][1 + layer], b * P:(b + 1) * P], xn[layer][:, t, :], ident)
                last.then_inc(xnT_ready, 1)

            def cross_q(f):
                pe.wait_ge(xnT_copied, NORMS.index((0, f)) + 1)
                mm(ps[:, BANKS[f][0], :], xw_sb[:, WQ, :], xnT[0][:, f * 512:(f + 1) * 512],
                   start=True, stop=True).then_inc(qT_ready, 1)

            def cross_scores(f):
                pe.wait_ge(qT_copied, f + 1)
                for b in range(B):
                    t = 4 * f + b
                    last = mm(ps[:, BANKS[f][2 + b // 2], b % 2 * S:(b % 2 + 1) * S], qT[:, t * P:(t + 1) * P],
                              kT[:, b * S:(b + 1) * S], start=True, stop=True)
                    if b % 2:
                        last.then_inc(xs_ready, 1)

            def turn_probabilities(f):
                for b in range(B):
                    t = 4 * f + b
                    pe.wait_ge(xs_exp, t + 1)
                    for jh in range(2):
                        last = turn(ps[:, BANKS[f][b // 2], (b % 2 * 2 + jh) * P:(b % 2 * 2 + jh + 1) * P],
                                    sc[:, t, jh * P:(jh + 1) * P], ident)
                    if b % 2:
                        last.then_inc(pT_ready, 1)

            def cross_values(f):
                pe.wait_ge(xv_biased, 2)
                for b in range(B):
                    pe.wait_ge(pT_copied, 2 * f + b // 2 + 1)
                    for jh in range(2):
                        last = mm(ps[:, BANKS[f][2], b * P:(b + 1) * P], v_nat[:, 2 * b + jh, :],
                                  pT[:, 4 * f + b, jh, :], start=(jh == 0), stop=(jh == 1))
                last.then_inc(cT_ready, 1)

            def cross_out(f):
                pe.wait_ge(cT_copied, f + 1)
                for b in range(B):
                    t = 4 * f + b
                    last = mm(ps[:, BANKS[f][3], b * D:(b + 1) * D], cT[:, t * P:(t + 1) * P], xw_sb[:, WO, :],
                              start=True, stop=True)
                last.then_inc(xatt_ready, 1)

            def gate(f, o):
                if f == 0 and o == 0:
                    pe.wait_ge(weights_cut, 1)
                if o == 0:
                    pe.wait_ge(x2_cut, f + 1)
                if o >= 2:
                    pe.wait_ge(gate_read, 4 * f + o - 1)
                for e, w in ((0, W1), (1, W2)):
                    for n, (m, a) in enumerate(PASSES):
                        last = mm(ps[:, BANKS[f][o % 2 * 2 + e], :], w_part[m][:, w + o * P:w + (o + 1) * P],
                                  x2T[:, a, f * 512:(f + 1) * 512], start=(n == 0), stop=(n == 2))
                last.then_inc(gate_ready, 1)

            def hidden(layer, f, o):
                w, given, ready = ((H1, gate_done, mid1_ready), (H2, mid1_cut, mid2_ready))[layer]
                if layer == 0 and o == 0:
                    pe.wait_ge(gate_read, NO * (f + 1))
                for k in range(NO):
                    c = w + k * HID + o * P
                    pe.wait_ge(given, NO * f + k + 1)
                    if k == 0 and f == 0 and o == 0:
                        pe.wait_ge(weights_cut, 2 + layer)
                    for n, (m, a) in enumerate(PASSES):
                        last = mm(ps[:, BANKS[f][o], :], w_part[m][:, c:c + P], hid[:, layer, f, a, k, :],
                                  start=(k == 0 and n == 0), stop=(k == NO - 1 and n == 2))
                last.then_inc(ready, 1)

            def network_out(f):
                if f == 0:
                    pe.wait_ge(w3_scaled, 1)
                for b in range(B):
                    for k in range(NO):
                        if b == 0:
                            pe.wait_ge(mid2_done, NO * f + k + 1)
                        last = mm(ps[:, BANKS[f][b // 2], b % 2 * D:(b % 2 + 1) * D],
                                  hid3[:, f, k, b * P:(b + 1) * P], w3_sb[:, k, :],
                                  start=(k == 0), stop=(k == NO - 1))
                    if b % 2:
                        last.then_inc(ffn_ready, 1)

            pe.wait_ge(ld_rv, 16)
            for job in range(4):
                relative_values(job)
            scores(*LAST_UNITS[0])
            turn_relative_values(0)
            scores(*LAST_UNITS[1])
            values(*LAST_UNITS[0])
            turn_heads(0)
            scores(*LAST_UNITS[2])
            values(*LAST_UNITS[1])
            scores(*LAST_UNITS[3])
            attention_out(0)
            values(*LAST_UNITS[2])
            values(*LAST_UNITS[3])
            turn_x(0, 0)
            relative_values(4)
            cross_q(0)
            cross_scores(0)
            relative_values(5)
            turn_probabilities(0)
            relative_values(6)
            cross_values(0)
            cross_out(0)
            relative_values(7)
            turn_relative_values(1)
            turn_x(1, 0)
            turn_heads(1)
            gate(0, 0)
            attention_out(1)
            gate(0, 1)
            gate(0, 2)
            turn_x(0, 1)
            gate(0, 3)
            cross_q(1)
            cross_scores(1)
            hidden(0, 0, 0)
            hidden(0, 0, 1)
            turn_probabilities(1)
            hidden(0, 0, 2)
            cross_values(1)
            cross_out(1)
            hidden(0, 0, 3)
            hidden(1, 0, 0)
            turn_x(1, 1)
            hidden(1, 0, 1)
            gate(1, 0)
            gate(1, 1)
            hidden(1, 0, 2)
            gate(1, 2)
            gate(1, 3)
            hidden(1, 0, 3)
            for o in range(NO):
                hidden(0, 1, o)
            network_out(0)
            for o in range(NO):
                hidden(1, 1, o)
            network_out(1)

        @block.scalar
        def _(act):
            run = nc.scalar.activation

            act.wait_ge(ld_table, 16 * N_TABLE)
            for half in range(2):
                act.wait_ge(proj_ready, 2 * half + 1)
                run(q_part[:, half, 0, :], ps[:, 2 * half, :], ACT.Copy).then_inc(upper_done, 1)
                act.wait_ge(proj_ready, 2 * half + 2)
                for side, bias in ((1, con[:, FIRST:FIRST + 1]), (0, con[:, LAST:LAST + 1])):
                    run(k_part[:, side, half, 0, :], ps[:, 2 * half + 1, :], ACT.Identity,
                        bias=bias).then_inc(upper_done, 1)

            act.wait_ge(ld_cross, 16 * N_CROSS)
            for n in range(2):
                act.wait_ge(kT_ready, n + 1)
                run(kT[:, n * 512:(n + 1) * 512], ps[:, 6 + n, :], ACT.Identity,
                    bias=cols[:, COL_XBK:COL_XBK + 1]).then_inc(kT_copied, 1)

            act.wait_ge(ones_set, 1)
            for n in range(2 * B):
                b, side = n // 2, n % 2
                act.wait_ge(v_ready, n + 1)
                for half in range(2):
                    last = run(vw_at[:, b, side, half, :, :, 0:DK].rearrange("p h e d -> p e h d"),
                               ps[:, 4 + side, half * S:(half + 1) * S].rearrange("p (e h d) -> p e h d", e=2, h=H),
                               ACT.Copy)
                last.then_inc(v_copied[side], 1)
            for n in range(2):
                act.wait_ge(xv_ready, n + 1)
                run(v_nat[:, 4 * n:4 * n + 4, :].rearrange("p t d -> p (t d)"), ps[:, 4 + n, :],
                    ACT.Copy).then_inc(xv_copied, 1)

            def copy_maxima(b):
                act.wait_ge(negm_turned, b + 1)
                run(mt[:, b, :], ps[0:3 * H, 2, 0:S], ACT.Copy).then_inc(negm_copied, 1)

            for n in range(S // 8):
                if n == sum(REL_AFTER[:2 * G]):
                    copy_maxima(0)
                act.wait_ge(rel_ready, n + 1)
                run(near[:, 8 * n:8 * n + 8, :].rearrange("p i m -> p (i m)"), ps[:, 4 + n % 4, :],
                    ACT.Copy).then_inc(rel_copied, 1)

            def probabilities(q, b, half, g):
                act.wait_ge(far_ready, q + 1)
                if q >= 2:
                    act.wait_ge(pv_done, q - 1)
                run(far[:, q % 2, :], ps[:, 5 + q % 2, :], ACT.Exp, scale=float(DK) ** -0.5).then_inc(exp_far, 1)
                act.wait_ge(near_added, q + 1)
                tile = heads_of(near, b, half, g)
                run(tile, tile, ACT.Exp, scale=float(DK) ** -0.5).then_inc(exp_near, 1)
                if maxima_at(q) is not None:
                    copy_maxima(maxima_at(q))

            for q, b, half, g in list(units())[:FIRST_UNITS]:
                probabilities(q, b, half, g)

            def odd_values(job):
                act.wait_ge(relv_ready, job + 1)
                run(rvo[:, 32 * job + 1:32 * (job + 1):2, :],
                    ps[BH:P, REL_BANK[job], 0:32 * DK].rearrange("p (i e d) -> p i e d", e=2, d=DK)[:, :, 0, :],
                    ACT.Copy).then_inc(relv_odd, 1)

            def copy_half(to, f, bank, ready, count, done, bias=None):
                act.wait_ge(ready, count)
                o, i = to[:, f * 512:(f + 1) * 512], ps[:, BANKS[f][bank], :]
                if bias is None:
                    run(o, i, ACT.Copy).then_inc(done, 1)
                else:
                    run(o, i, ACT.Identity, bias=bias).then_inc(done, 1)

            def copy_heads(f):
                copy_half(cattT, f, 1, cattT_ready, f + 1, cattT_copied)

            def copy_x(layer, f):
                copy_half(xnT[layer], f, 1 + layer, xnT_ready, NORMS.index((layer, f)) + 1, xnT_copied)

            def copy_q(f):
                copy_half(qT, f, 0, qT_ready, f + 1, qT_copied, cols[:, COL_XBQ:COL_XBQ + 1])

            def cross_exp(f):
                for t in range(4 * f, 4 * f + 4):
                    act.wait_ge(xs_max, t // 2 + 1)
                    run(sc[:, t, :], sc[:, t, :], ACT.Exp, bias=smax[:, t:t + 1],
                        accum_out=ssum[:, t:t + 1]).then_inc(xs_exp, 1)

            def copy_probabilities(f):
                for n in range(2):
                    act.wait_ge(pT_ready, 2 * f + n + 1)
                    t = 4 * f + 2 * n
                    run(pT[:, t:t + 2, :, :].rearrange("p t j i -> p (t j i)"), ps[:, BANKS[f][n], :],
                        ACT.Copy).then_inc(pT_copied, 1)

            def copy_context(f):
                copy_half(cT, f, 2, cT_ready, f + 1, cT_copied)

            def silu_gate(f, o):
                n = NO * f + o
                act.wait_ge(gate_ready, n + 1)
                if n >= 2:
                    act.wait_ge(gate_done, n - 1)
                run(silu[:, n % 2, :], ps[:, BANKS[f][o % 2 * 2], :], ACT.Silu,
                    scale=cols[:, COL_S1 + o:COL_S1 + o + 1]).then_inc(silu_done, 1)

            def gelu(layer, f, o):
                ready, done, c = ((mid1_ready, mid1_done, COL_H1), (mid2_ready, mid2_done, COL_H2))[layer]
                act.wait_ge(ready, NO * f + o + 1)
                if layer == 0 and f == 1:
                    act.wait_ge(mid1_cut, o + 1)
                dst = gelu_out[:, o, :] if layer == 0 else hid3[:, f, o, :]
                run(dst, ps[:, BANKS[f][o], :], ACT.Gelu,
                    scale=cols[:, c + o:c + o + 1]).then_inc(done, 1)

            for job in range(4):
                odd_values(job)
            probabilities(*LAST_UNITS[0])
            probabilities(*LAST_UNITS[1])
            copy_heads(0)
            probabilities(*LAST_UNITS[2])
            probabilities(*LAST_UNITS[3])
            copy_x(0, 0)
            odd_values(4)
            copy_q(0)
            cross_exp(0)
            odd_values(5)
            copy_probabilities(0)
            odd_values(6)
            copy_context(0)
            odd_values(7)
            copy_x(1, 0)
            copy_heads(1)
            silu_gate(0, 0)
            silu_gate(0, 1)
            silu_gate(0, 2)
            copy_x(0, 1)
            silu_gate(0, 3)
            copy_q(1)
            cross_exp(1)
            gelu(0, 0, 0)
            gelu(0, 0, 1)
            copy_probabilities(1)
            gelu(0, 0, 2)
            copy_context(1)
            gelu(0, 0, 3)
            copy_x(1, 1)
            for o in range(NO):
                silu_gate(1, o)
            for layer, f in ((1, 0), (0, 1), (1, 1)):
                for o in range(NO):
                    gelu(layer, f, o)

        @block.gpsimd
        def _(pool):
            nc.gpsimd.memset(vw[:], 1.0).then_inc(ones_set, 1)
            nc.gpsimd.memset(q_st[:, Q_ZERO:].rearrange("p a e b i -> p (a e b i)").bitcast(F32), 0.0
                             ).then_inc(zeros_set_pool, 1)
            for k in k_st:
                nc.gpsimd.memset(k[:].rearrange("p a b j -> p (a b j)").bitcast(F32), BF16_ONES).then_inc(k_ones_set, 1)
            nc.gpsimd.memset(half_pow[:], -0.5).then_inc(pool_step, 1)
            pool.wait_ge(ld_relv, 16)
            for b in range(B):
                pool.wait_ge(v_copied[1], b + 1)
                for half in range(2):
                    there = vw_at[:, b, 1, half, :, :, 0:DK]
                    last = nc.gpsimd.tensor_tensor(
                        there, there, rvfar[:, 2 * half:2 * half + 2, :].unsqueeze(1).to_broadcast([P, H, 2, DK]),
                        ALU.add)
                last.then_inc(far_valued, 1)
            pool.wait_ge(ld_cross, 16 * N_CROSS)
            for n in range(2):
                pool.wait_ge(xv_copied, n + 1)
                there = v_nat[:, 4 * n:4 * n + 4, :]
                nc.gpsimd.tensor_tensor(there, there, rows[:, ROW_XBV:ROW_XBV + 1, :].to_broadcast([P, 4, D]),
                                        ALU.add).then_inc(xv_biased, 1)
            pool.wait_ge(pool_step, 1)

            def reciprocal_deviation(layer, f):
                for p in range(2):
                    n, t = 2 * NORMS.index((layer, f)) + p, slice(4 * f + 2 * p, 4 * f + 2 * p + 2)
                    pool.wait_ge(ln_var, n + 1)
                    r = rstd[:, layer, t]
                    nc.gpsimd.tensor_scalar(r, mv[:, layer, t, 1], EPS, None, ALU.add).then_inc(pool_step, 1)
                    pool.wait_ge(pool_step, 2 + n)
                    nc.gpsimd.tensor_tensor(r, r, half_pow[:, t], ALU.pow).then_inc(ln_rstd, 1)

            pool.wait_ge(ld_x_nat, 16 * 2)
            nc.gpsimd.tensor_tensor(xb[:, 0], xb[:, 0], rows[:, ROW_BO:ROW_BO + 1, :].to_broadcast([P, NT, D]),
                                    ALU.add).then_inc(xb_done, 1)

            def second_residual(f):
                pool.wait_ge(xn_done, 4 * NORMS.index((0, f)) + 4)
                t = slice(4 * f, 4 * f + 4)
                nc.gpsimd.tensor_tensor(xb[:, 1, t, :], xn[0][:, t, :],
                                        rows[:, ROW_XBO:ROW_XBO + 1, :].to_broadcast([P, 4, D]),
                                        ALU.add).then_inc(xb_done, 1)

            def turn_mask(f):
                pool.wait_ge(ld_mask[f], 16)
                nc.gpsimd.tensor_scalar(pen[f], mask_in[f], 0.0, NEG, ALU.is_equal, ALU.mult
                                        ).then_inc(mask_turned, 1)

            turn_mask(0)
            reciprocal_deviation(0, 0)
            second_residual(0)
            turn_mask(1)
            reciprocal_deviation(1, 0)
            reciprocal_deviation(0, 1)
            second_residual(1)
            pool.wait_ge(ld_w3, 16)
            nc.gpsimd.tensor_tensor(w3_sb[:], w3_sb[:], rows[:, ROW_S3:ROW_S3 + 1, :].to_broadcast([P, NO, D]),
                                    ALU.mult).then_inc(w3_scaled, 1)
            for layer, f in NORMS[3:]:
                reciprocal_deviation(layer, f)

        @block.vector
        def _(dve):
            v = nc.vector
            steps = [0]

            def settle(ins):
                steps[0] += 1
                ins.then_inc(dve_step, 1)
                dve.wait_ge(dve_step, steps[0])

            def col(c):
                return con[:, c:c + 1]

            v.memset(q_st[:, 0:Q_ZERO].rearrange("p a e b i -> p (a e b i)").bitcast(F32), 0.0).then_inc(zeros_set, 1)

            def cut_parts(whole, rest, parts):
                settle(v.tensor_copy(parts[0], whole))
                settle(v.tensor_tensor(rest, whole, parts[0], ALU.subtract))
                settle(v.tensor_copy(parts[1], rest))
                return v.tensor_tensor(parts[2], rest, parts[1], ALU.subtract)

            def cut_projection(c):
                what, side, half = CUTS[c]
                if what == "q":
                    dve.wait_ge(upper_done, 3 * half + 1)
                    parts = [q_part[:, half, m, :] for m in range(3)]
                    settle(v.tensor_tensor(left[:, c % 2, :], ps[:, 2 * half, :], parts[0], ALU.subtract))
                else:
                    dve.wait_ge(upper_done, 3 * half + 3)
                    parts = [k_part[:, side, half, m, :] for m in range(3)]
                    settle(v.scalar_tensor_tensor(left[:, c % 2, :], ps[:, 2 * half + 1, :], col((LAST, FIRST)[side]),
                                                  parts[0], ALU.add, ALU.subtract))
                settle(v.tensor_copy(parts[1], left[:, c % 2, :]))
                v.tensor_tensor(parts[2], left[:, c % 2, :], parts[1], ALU.subtract).then_inc(parts_done, 1)

            def cut_table():
                settle(v.tensor_scalar(cut[:, 0, :], relraw[:], relraw[:, 0:1], None, ALU.subtract))
                settle(cut_parts(cut[:, 0, :], cut[:, 1, :], [cut_bf[:, 0, :], cut_bf[:, 1, :], cut[:, 2, :]]))
                settle(v.tensor_scalar(cut[:, 3, :], cut_bf[:, 0, :], col(HI), None, ALU.mult))
                settle(v.scalar_tensor_tensor(cut[:, 4, :], cut_bf[:, 1, :], col(MID), cut[:, 3, :], ALU.mult, ALU.add))
                v.scalar_tensor_tensor(table[:], cut[:, 2, :], col(LO), cut[:, 4, :],
                                       ALU.mult, ALU.add).then_inc(table_done, 1)

            dve.wait_ge(ld_table, 16 * N_TABLE)
            for c in range(len(CUTS)):
                cut_projection(c)
                if c == 2:
                    cut_table()

            def maxima(b, half, g):
                u = (2 * b + half) * G + g
                for pair in range(2):
                    n, h = 2 * u + pair, K4 * g + 2 * pair
                    dve.wait_ge(nat_ready, n + 1)
                    v.tensor_reduce(mq[:, half, b, h:h + 2], ps[:, n % 2, :].rearrange("p (h j) -> p h j", h=2),
                                    AX.X, ALU.max).then_inc(nat_read, 1)
                dve.wait_ge(dist_ready, u + 1)
                v.tensor_reduce(mr[:, half, b, K4 * g:K4 * g + K4],
                                ps[:, 2, 0:K4 * 66].rearrange("p (h r) -> p h r", h=K4),
                                AX.X, ALU.max).then_inc(dist_read, 1)

            def shift(b):
                dve.wait_ge(dist_read, 8 * (b + 1))
                settle(v.scalar_tensor_tensor(negm[:, :, b, :], mq[:, :, b, :], -1.0, mr[:, :, b, :],
                                              ALU.mult, ALU.subtract))
                st = [negm_st[:, :, b, m * H:(m + 1) * H].rearrange("p f (e a) -> p f a e", e=2) for m in range(3)]

                def by_pair(t):
                    return t.rearrange("p f (a e) -> p f a e", e=2)

                whole, rest = negm[:, :, b, :], negm_left[:, :, b, :]
                bf = [negm_bf[:, m, :, b, :] for m in range(2)]
                settle(cut_parts(whole, rest, [bf[0], bf[1], negm[:, :, b, :]]))
                v.tensor_copy(st[0], by_pair(bf[0]))
                v.tensor_copy(st[1], by_pair(bf[1]))
                settle(v.tensor_copy(st[2], by_pair(negm[:, :, b, :])))
                dve.nop().then_inc(negm_done, 1)

            def add_relative(q, b, half, g):
                dve.wait_ge(near_ready, q + 1)
                if q == 0:
                    dve.wait_ge(rel_copied, S // 8)
                tile = heads_of(near, b, half, g)
                v.tensor_tensor(tile, ps[:, 3 + q % 2, :].rearrange("p (k i) -> p k i", k=K4), tile,
                                ALU.add).then_inc(near_added, 1)

            def copy_values(q, b, half):
                dve.wait_ge(pv_done, q + 1)
                for e in range(2):
                    r = slice(e * BLK, (e + 1) * BLK)
                    last = v.tensor_copy(pvs[r, half, b * H:(b + 1) * H, :],
                                         ps[r, 7, 0:2 * VC * H].rearrange("p (h e d) -> p h e d", e=2, d=VC)[:, :, e, :])
                last.then_inc(pv_copied, 1)

            for u in range(AHEAD):
                maxima(*natural_unit(u))
                if u == 2 * G - 1:
                    shift(0)
            for q, b, half, g in list(units())[:FIRST_UNITS]:
                if q % G == 1 and q > G:
                    copy_values(q - 2, (q - 2) // 8, (q - 2) // G % 2)
                add_relative(q, b, half, g)
                if maxima_at(q) is not None:
                    shift(maxima_at(q))
                if q + AHEAD < 4 * 8:
                    maxima(*natural_unit(q + AHEAD))
            copy_values(FIRST_UNITS - 1, B - 1, 0)

            def even_values(job):
                dve.wait_ge(relv_ready, job + 1)
                v.tensor_copy(rvo[:, 32 * job:32 * (job + 1):2, :],
                              ps[0:BH, REL_BANK[job], 0:32 * DK].rearrange("p (i e d) -> p i e d", e=2, d=DK)[:, :, 1, :]
                              ).then_inc(relv_even, 1)

            def heads_out(f):
                dve.wait_ge(relv_turned, f + 1)
                for b in range(B):
                    turned = ps[:, BANKS[f][0], :].rearrange("p (d h b) -> p b h d", d=DK, b=B)[:, b]
                    last = v.tensor_tensor(catt[:, f, b * H:(b + 1) * H, :], turned,
                                           pvs[:, f, b * H:(b + 1) * H, 0:DK], ALU.add)
                settle(last)
                v.tensor_tensor(catt[:, f], catt[:, f], lsum[:, f, :].unsqueeze(2).to_broadcast([P, BH, DK]),
                                ALU.mult).then_inc(catt_done, 1)

            def moments(layer, f):
                ready, bank, base = ((att_ready, 0, xb[:, 0]), (xatt_ready, 3, xb[:, 1]),
                                     (ffn_ready, 0, xn[1]))[layer]
                t0 = slice(4 * f, 4 * f + 4)
                if layer == 0:
                    dve.wait_ge(xb_done, 1)
                if layer == 1:
                    dve.wait_ge(xb_done, 2 + f)
                    dve.wait_ge(xs_exp, 4 * f + 4)
                    settle(v.reciprocal(srec[:, t0], ssum[:, t0]))
                if layer < 2:
                    dve.wait_ge(ready, f + 1)
                src = ps[:, BANKS[f][bank], :].rearrange("p (t d) -> p t d", t=4)
                if layer == 0:
                    settle(v.tensor_tensor(y[:, t0, :], src, base[:, t0, :], ALU.add))
                for p in range(2):
                    two = slice(4 * f + 2 * p, 4 * f + 2 * p + 2)
                    if layer == 1:
                        for b in range(2 * p, 2 * p + 2):
                            t = 4 * f + b
                            last = v.scalar_tensor_tensor(y[:, t, :], src[:, b, :], srec[:, t:t + 1], base[:, t, :],
                                                          ALU.mult, ALU.add)
                        settle(last)
                    if layer == 2:
                        dve.wait_ge(ready, 2 * f + p + 1)
                        settle(v.tensor_tensor(y[:, two, :],
                                               ps[:, BANKS[f][p], 0:2 * D].rearrange("p (t d) -> p t d", t=2),
                                               base[:, two, :], ALU.add))
                    for t in range(two.start, two.stop):
                        last = v.bn_stats(stats[:, t, :], y[:, t, :])
                    settle(last)
                    for t in range(two.start, two.stop):
                        last = v.bn_aggr(mv[:, layer, t, :], stats[:, t, :])
                    last.then_inc(ln_var, 1)

            def normed(layer, f):
                for p in range(2):
                    dve.wait_ge(ln_rstd, 2 * NORMS.index((layer, f)) + p + 1)
                    for t in range(4 * f + 2 * p, 4 * f + 2 * p + 2):
                        v.tensor_scalar(xn[layer][:, t, :], y[:, t, :], mv[:, layer, t, 0:1],
                                        rstd[:, layer, t:t + 1], ALU.subtract, ALU.mult).then_inc(xn_done, 1)

            def norm(layer, f):
                moments(layer, f)
                normed(layer, f)

            def mask_scores(f, n):
                dve.wait_ge(mask_turned, f + 1)
                dve.wait_ge(xs_ready, 2 * f + n + 1)
                two = slice(4 * f + 2 * n, 4 * f + 2 * n + 2)
                settle(v.scalar_tensor_tensor(
                    sc[:, two, :], ps[:, BANKS[f][2 + n], :].rearrange("p (t j) -> p t j", t=2),
                    float(D) ** -0.5, pen[f][:, 2 * n:2 * n + 2, :], ALU.mult, ALU.add))
                v.tensor_reduce(smax[:, two], sc[:, two, :], AX.X, ALU.max, negate=True).then_inc(xs_max, 1)

            def cut_in_two(whole, upper, lower):
                settle(v.tensor_copy(upper, whole))
                return v.tensor_tensor(lower, whole, upper, ALU.subtract)

            def cut_weights(c0, c1):
                return cut_in_two(w_whole[:, c0:c1], w_part[0][:, c0:c1], w_part[1][:, c0:c1])

            def cut_x(f):
                dve.wait_ge(xnT_copied, NORMS.index((1, f)) + 1)
                t = slice(f * 512, (f + 1) * 512)
                cut_in_two(xnT[1][:, t], x2T[:, 0, t], x2T[:, 1, t]).then_inc(x2_cut, 1)

            def gated(f, o):
                n = NO * f + o
                dve.wait_ge(silu_done, n + 1)
                both = silu[:, n % 2, :]
                v.scalar_tensor_tensor(both, ps[:, BANKS[f][o % 2 * 2 + 1], :],
                                       cols[:, COL_S2 + o:COL_S2 + o + 1], both,
                                       ALU.mult, ALU.mult).then_inc(gate_read, 1)
                dve.wait_ge(gate_read, n + 1)
                cut_in_two(both, hid[:, 0, f, 0, o, :], hid[:, 0, f, 1, o, :]).then_inc(gate_done, 1)

            def cut_hidden(f, o):
                dve.wait_ge(mid1_done, NO * f + o + 1)
                cut_in_two(gelu_out[:, o, :], hid[:, 1, f, 0, o, :], hid[:, 1, f, 1, o, :]).then_inc(mid1_cut, 1)

            dve.wait_ge(pv_copied, 2 * B - 1)
            for job in range(4):
                even_values(job)
                if job == 0:
                    settle(v.reciprocal(lsum[:, 0], pvs[:, 0, :, DK]))
            add_relative(*LAST_UNITS[0])
            heads_out(0)
            for u in LAST_UNITS[1:]:
                add_relative(*u)
            norm(0, 0)
            copy_values(4 * 8 - 1, B - 1, 1)
            dve.wait_ge(pv_copied, 2 * B)
            settle(v.reciprocal(lsum[:, 1], pvs[:, 1, :, DK]))
            even_values(4)
            mask_scores(0, 0)
            mask_scores(0, 1)
            even_values(5)
            dve.wait_ge(ld_gates, 16 * 2)
            cut_weights(W1, H1).then_inc(weights_cut, 1)
            even_values(6)
            dve.wait_ge(ld_h1, 16)
            cut_weights(H1, H1 + 2 * HID)
            moments(1, 0)
            even_values(7)
            normed(1, 0)
            heads_out(1)
            cut_x(0)
            cut_weights(H1 + 2 * HID, H2).then_inc(weights_cut, 1)
            moments(0, 1)
            gated(0, 0)
            normed(0, 1)
            gated(0, 1)
            gated(0, 2)
            gated(0, 3)
            mask_scores(1, 0)
            mask_scores(1, 1)
            dve.wait_ge(ld_h2, 16)
            cut_weights(H2, H2 + 2 * HID)
            cut_hidden(0, 0)
            cut_hidden(0, 1)
            cut_weights(H2 + 2 * HID, W_ALL).then_inc(weights_cut, 1)
            cut_hidden(0, 2)
            moments(1, 1)
            cut_hidden(0, 3)
            normed(1, 1)
            cut_x(1)
            for o in range(NO):
                gated(1, o)
            for o in range(NO):
                cut_hidden(1, o)
            norm(2, 0)
            norm(2, 1)


def kernel(**inputs):
    import numpy as np
    import concourse.bacc as bacc
    from concourse.bass_utils import run_bass_kernel_spmd

    a = {k.replace("L0_", ""): np.asarray(v) for k, v in inputs.items()}
    tokens = a["x"].reshape(TOK, D)
    around = [j % S for j in range(HALO)]
    clipped = [min(max(u - (P - 1), -MAX_REL), MAX_REL) + MAX_REL for u in range(2 * P + WIDE // DK)]
    far_rows = [[(0 if (w + P) + c >= S else NREL - 1) for w in WIN] for c in range(P)]
    consts = np.zeros((P, P + 8), np.float32)
    consts[:, :P] = np.eye(P, dtype=np.float32)
    consts[:, LAST] = np.repeat(a["attn_rel_k_emb"][-1], H)
    consts[:, FIRST] = np.repeat(a["attn_rel_k_emb"][0], H)
    for r in range(P):
        if r % BLK < SHIFT:
            consts[r, HI + STACK[r % BLK // DK][1]] = 1

    def columns(s):
        return s.reshape(-1, P).T

    def side_by_side(*weights):
        return np.stack([a[w].T for w in weights], 1)

    order = np.arange(D).reshape(PAIRS, 2, DK).transpose(2, 1, 0).reshape(-1)
    w_self = side_by_side("attn_Wq", "attn_Wk", "attn_Wv", "attn_Wo")
    w_self[:, :WV] = w_self[:, :WV, order]
    arrays = dict(
        x=tokens, xT=a["x"].transpose(2, 0, 1)[:, :, around],
        ctxT=a["ctx_1024"].reshape(TOK, D).T, mask=a["mask_BxSxS2_if1"].reshape(TOK, S),
        consts=consts,
        w_self=w_self,
        relk=np.tile(a["attn_rel_k_emb"][clipped[:2 * P]].T, (H, 1)),
        relv=a["attn_rel_v_emb"][clipped], relv_far=a["attn_rel_v_emb"][far_rows],
        w_cross=side_by_side("xattn_Wq", "xattn_Wk", "xattn_Wv", "xattn_Wo"),
        vectors=np.stack([a["attn_b_o"], a["xattn_bv"], a["xattn_bo"], a["ffn_w3_s"]]),
        columns=np.concatenate([columns(a[n]) for n in (
            "xattn_bq", "xattn_bk", "ffn_w1_s", "ffn_w2_s", "ffn_h1_s", "ffn_h2_s")], 1),
        w1=a["ffn_w1_w"].T, w2=a["ffn_w2_w"].T, h1=a["ffn_h1_w"].T, h2=a["ffn_h2_w"].T, w3=a["ffn_w3_w"].T)
    arrays = {k: np.ascontiguousarray(v) for k, v in arrays.items()}

    nc = bacc.Bacc("TRN2", target_bir_lowering=False, num_devices=1)
    ap = {k: nc.dram_tensor("in_" + k, v.shape, mybir.dt.from_np(v.dtype), kind="ExternalInput").ap()
          for k, v in arrays.items()}
    result = nc.dram_tensor("out", (TOK, D), F32, kind="ExternalOutput").ap()
    build(nc, *(ap.get(n) for n in (
        "x", "xT", "ctxT", "mask", "consts", "w_self", "relk", "relv", "relv_far",
        "w_cross", "vectors", "columns", "w1", "w2", "h1", "h2", "w3")), result)
    r = run_bass_kernel_spmd(nc, [{"in_" + k: v for k, v in arrays.items()}], core_ids=[0])
    return r.results[0]["out"].reshape(B, S, D)
```
